# Optimizing a Trainium2 kernel written in Bass

```python
import numpy as np
import jax
import jax.numpy as jnp

def _softmax(x, axis=-1):
    return jax.nn.softmax(x, axis=axis)

def _gelu(x):
    return jax.nn.gelu(x, approximate=True)

def _silu(x):
    return jax.nn.silu(x)

def _sigmoid(x):
    return jax.nn.sigmoid(x)

def _layernorm(x, axis=-1, eps=1e-05):
    m = jnp.mean(x, axis=axis, keepdims=True)
    v = jnp.var(x, axis=axis, keepdims=True)
    return (x - m) / jnp.sqrt(v + eps)

def _scatter_add(tgt, idx, src, axis=0):
    return tgt.at[idx].add(src)

def _segment_sum(src, seg, n):
    return jax.ops.segment_sum(src, seg, n)
kernel_name = 'mk_adaln_ffn_d2_seqx_r8_5cb313'

def setup_inputs(seed: int=0):
    np.random.seed(seed)
    _w = jnp.asarray

    def _rec_inputs():
        import jax
        import jax.numpy as jnp
        _rk = jax.random.key(seed)
        x = 7.22e-05 + 1 * jax.random.normal(jax.random.fold_in(_rk, 1), (8, 128, 512), jnp.float32)
        _lenS = 128 - jax.random.randint(jax.random.fold_in(_rk, 7), (8,), 0, max(1, 128 // 4) + 1, jnp.int32)
        _lenS2 = 128 - jax.random.randint(jax.random.fold_in(_rk, 8), (8,), 0, max(1, 128 // 4) + 1, jnp.int32)
        itok_B_2_6 = jax.random.randint(jax.random.fold_in(_rk, 11), (8,), 2, 7, jnp.int32)
        condB_coeff = 0.00219231 + 0.0100837 * jax.random.normal(jax.random.fold_in(_rk, 12), (8,), jnp.float32)
        _validS = jnp.arange(128)[None, :] < _lenS[:, None]
        _validS2 = jnp.arange(128)[None, :] < _lenS2[:, None]
        _causal = jnp.tril(jnp.ones((128, 128), dtype=bool))
        mask_Bx4096x4096_ik1 = jnp.where(jnp.ones((8, 512, 512), dtype=bool), 1, 0).astype(jnp.int32)
        return (x, itok_B_2_6, condB_coeff, mask_Bx4096x4096_ik1)
    x, itok_B_2_6, condB_coeff, mask_Bx4096x4096_ik1 = _rec_inputs()

    def _L0_cond_setup():
        import jax, jax.numpy as jnp
        import numpy as np
        B, N, H, F = (4, 64, 512, 1376)
        L, R, RANK = (1, 16, 16)
        SCALE = 0.5
        key = jax.random.key(seed)
        ks = jax.random.split(key, 12)
        nrm = lambda k, shape, fan: jax.random.normal(k, shape, jnp.float32) * fan ** (-0.5)
        inp = {'x': jax.random.normal(ks[0], (B, N, H), jnp.float32), 'W_gate': nrm(ks[1], (F, H), H), 'W_up': nrm(ks[2], (F, H), H), 'W_down': nrm(ks[3], (H, F), F), 'A_gate': nrm(ks[4], (L, R, RANK, H), H), 'B_gate': nrm(ks[5], (L, R, F, RANK), RANK), 'A_up': nrm(ks[6], (L, R, RANK, H), H), 'B_up': nrm(ks[7], (L, R, F, RANK), RANK), 'A_down': nrm(ks[8], (L, R, RANK, F), F), 'B_down': nrm(ks[9], (L, R, H, RANK), RANK), 'lora_indices': jax.random.randint(ks[10], (B,), 0, R), 'layer_idx': 0}
        return inp
    _L0_cond_all = _L0_cond_setup()
    _L0_cond_in = {k: v for k, v in _L0_cond_all.items() if k in ('W_gate', 'W_up', 'W_down', 'A_gate', 'B_gate', 'A_up', 'B_up', 'A_down', 'B_down')}
    del _L0_cond_all

    def _L0_ffn_setup():
        import jax, jax.numpy as jnp
        import numpy as np
        B_, S, D_IN, D_OUT = (4, 256, 512, 512)
        N, RANK, ALPHA = (8, 16, 32)
        SCALE = ALPHA / RANK
        key = jax.random.key(seed)
        kx, ka, kb, kw, kbias = jax.random.split(key, 5)
        x = jax.random.normal(kx, (B_, S, D_IN), dtype=jnp.float32)
        lora_A = jax.random.normal(ka, (N, RANK, D_IN), dtype=jnp.float32) * (1.0 / np.sqrt(D_IN))
        lora_B = jax.random.normal(kb, (N, D_OUT, RANK), dtype=jnp.float32) * (1.0 / np.sqrt(RANK))
        W = jax.random.normal(kw, (D_OUT, D_IN), dtype=jnp.float32) * (1.0 / np.sqrt(D_IN))
        bias = jax.random.normal(kbias, (D_OUT,), dtype=jnp.float32) * 0.01
        lora_weights = jnp.full((N,), 1.0 / N, dtype=jnp.float32)
        return {'x': x, 'lora_A': lora_A, 'lora_B': lora_B, 'W': W, 'bias': bias, 'lora_weights': lora_weights}
    _L0_ffn_all = _L0_ffn_setup()
    _L0_ffn_in = {k: v for k, v in _L0_ffn_all.items() if k in ('lora_A', 'lora_B', 'W', 'bias', 'lora_weights')}
    del _L0_ffn_all

    def _L1_cond_setup():
        import jax, jax.numpy as jnp
        import numpy as np
        B, S, D_IN, D_OUT = (4, 64, 512, 512)
        key = jax.random.key(seed)
        k1, k2, k3, k4, k5 = jax.random.split(key, 5)
        hidden_states = jax.random.normal(k1, (B, S, D_IN), dtype=jnp.float32)
        W = jax.random.normal(k2, (D_OUT, D_IN), dtype=jnp.float32) * 0.02
        b = jax.random.normal(k3, (D_OUT,), dtype=jnp.float32) * 0.02
        coeff = jax.random.normal(k4, (B,), dtype=jnp.float32) * 0.01
        mask = jax.random.randint(k5, (B, D_IN, D_OUT), 0, 2, dtype=jnp.int32)
        return {'hidden_states': hidden_states, 'W': W, 'b': b, 'coeff': coeff, 'mask': mask}
    _L1_cond_all = _L1_cond_setup()
    _L1_cond_in = {k: v for k, v in _L1_cond_all.items() if k in ('W', 'b')}
    del _L1_cond_all

    def _L1_ffn_setup():
        import jax, jax.numpy as jnp
        import numpy as np
        BATCH, SEQ, D = (2, 256, 512)
        K, TOPK, RANK = (64, 16, 16)
        ALPHA = 32.0
        SCALING = ALPHA / RANK
        key = jax.random.key(seed)
        k1, k2, k3, k4 = jax.random.split(key, 4)
        x = jax.random.normal(k1, (BATCH, SEQ, D), dtype=jnp.float32)
        A = jax.random.normal(k2, (K, RANK, D), dtype=jnp.float32) * 0.02
        B = jax.random.normal(k3, (K, D, RANK), dtype=jnp.float32) * 0.02
        Wr = jax.random.normal(k4, (K, D), dtype=jnp.float32) * 0.02
        return {'x': x, 'A': A, 'B': B, 'Wr': Wr}
    _L1_ffn_all = _L1_ffn_setup()
    _L1_ffn_in = {k: v for k, v in _L1_ffn_all.items() if k in ('A', 'B', 'Wr')}
    del _L1_ffn_all
    return {'x': x, 'itok_B_2_6': itok_B_2_6, 'condB_coeff': condB_coeff, 'mask_Bx4096x4096_ik1': mask_Bx4096x4096_ik1, 'L0_cond_W_gate': _L0_cond_in['W_gate'], 'L0_cond_W_up': _L0_cond_in['W_up'], 'L0_cond_W_down': _L0_cond_in['W_down'], 'L0_cond_A_gate': _L0_cond_in['A_gate'], 'L0_cond_B_gate': _L0_cond_in['B_gate'], 'L0_cond_A_up': _L0_cond_in['A_up'], 'L0_cond_B_up': _L0_cond_in['B_up'], 'L0_cond_A_down': _L0_cond_in['A_down'], 'L0_cond_B_down': _L0_cond_in['B_down'], 'L0_ffn_lora_A': _L0_ffn_in['lora_A'], 'L0_ffn_lora_B': _L0_ffn_in['lora_B'], 'L0_ffn_W': _L0_ffn_in['W'], 'L0_ffn_bias': _L0_ffn_in['bias'], 'L0_ffn_lora_weights': _L0_ffn_in['lora_weights'], 'L1_cond_W': _L1_cond_in['W'], 'L1_cond_b': _L1_cond_in['b'], 'L1_ffn_A': _L1_ffn_in['A'], 'L1_ffn_B': _L1_ffn_in['B'], 'L1_ffn_Wr': _L1_ffn_in['Wr']}

def reference(x, itok_B_2_6, condB_coeff, mask_Bx4096x4096_ik1, L0_cond_W_gate, L0_cond_W_up, L0_cond_W_down, L0_cond_A_gate, L0_cond_B_gate, L0_cond_A_up, L0_cond_B_up, L0_cond_A_down, L0_cond_B_down, L0_ffn_lora_A, L0_ffn_lora_B, L0_ffn_W, L0_ffn_bias, L0_ffn_lora_weights, L1_cond_W, L1_cond_b, L1_ffn_A, L1_ffn_B, L1_ffn_Wr):
    import jax
    import jax.numpy as jnp

    def _L0_cond_ref(x, W_gate, W_up, W_down, A_gate, B_gate, A_up, B_up, A_down, B_down, lora_indices, layer_idx):
        import jax, jax.numpy as jnp
        import numpy as np
        B, N, H, F = (4, 64, 512, 1376)
        L, R, RANK = (1, 16, 16)
        SCALE = 0.5

        def lora_add(base, inp, A, B):
            Ab = A[layer_idx][lora_indices]
            Bb = B[layer_idx][lora_indices]
            t = jnp.einsum('bri,bni->bnr', Ab, inp)
            return base + jnp.einsum('bor,bnr->bno', Bb, t) * SCALE
        gate = lora_add(jnp.einsum('bnh,fh->bnf', x, W_gate), x, A_gate, B_gate)
        up = lora_add(jnp.einsum('bnh,fh->bnf', x, W_up), x, A_up, B_up)
        act = jax.nn.silu(gate) * up
        down = lora_add(jnp.einsum('bnf,hf->bnh', act, W_down), act, A_down, B_down)
        return down

    def _L0_ffn_ref(x, lora_A, lora_B, W, bias, lora_weights):
        import jax, jax.numpy as jnp
        import numpy as np
        B_, S, D_IN, D_OUT = (4, 256, 512, 512)
        N, RANK, ALPHA = (8, 16, 32)
        SCALE = ALPHA / RANK
        h = jnp.einsum('bsd,nrd->nbsr', x, lora_A)
        coef = (SCALE * lora_weights)[:, None, None]
        lora_out = jnp.einsum('nbsr,nor->bso', h, lora_B * coef)
        base = jnp.einsum('bsd,od->bso', x, W) + bias
        return base + lora_out

    def _L1_cond_ref(hidden_states, W, b, coeff, mask):
        import jax, jax.numpy as jnp
        import numpy as np
        B, S, D_IN, D_OUT = (4, 64, 512, 512)
        output = jnp.einsum('bsi,oi->bso', hidden_states, W) + b
        sign = (2 * mask - 1).astype(hidden_states.dtype)
        diff = jnp.einsum('bsi,bio->bso', hidden_states, sign)
        return output + diff * coeff[:, None, None]

    def _L1_ffn_ref(x, A, B, Wr):
        import jax, jax.numpy as jnp
        import numpy as np
        BATCH, SEQ, D = (2, 256, 512)
        K, TOPK, RANK = (64, 16, 16)
        ALPHA = 32.0
        SCALING = ALPHA / RANK
        prefix = x.shape[:-1]
        xf = x.reshape(-1, x.shape[-1])
        N = xf.shape[0]
        scores = xf @ Wr.T
        top_vals, top_idx = jax.lax.top_k(scores, TOPK)
        gates = jax.nn.softmax(top_vals, axis=-1)
        G = jnp.zeros((N, K), xf.dtype).at[jnp.arange(N)[:, None], top_idx].set(gates)
        h = jnp.einsum('nd,krd->nkr', xf, A)
        out = jnp.einsum('nkr,kdr->nd', h * G[:, :, None], B)
        return (out * SCALING).reshape(*prefix, -1)
    x = x + _L0_ffn_ref(_L0_cond_ref(x, L0_cond_W_gate, L0_cond_W_up, L0_cond_W_down, L0_cond_A_gate, L0_cond_B_gate, L0_cond_A_up, L0_cond_B_up, L0_cond_A_down, L0_cond_B_down, itok_B_2_6, 0), L0_ffn_lora_A, L0_ffn_lora_B, L0_ffn_W, L0_ffn_bias, L0_ffn_lora_weights)
    x = x + _L1_ffn_ref(_L1_cond_ref(x, L1_cond_W, L1_cond_b, condB_coeff, mask_Bx4096x4096_ik1), L1_ffn_A, L1_ffn_B, L1_ffn_Wr)
    return x

_drawn_inputs = setup_inputs


def setup_inputs(seed=0):
    import zlib

    import numpy as np

    out = dict(_drawn_inputs(seed))
    spreads = {'L0_ffn_lora_weights': (0.125, 0.2)}
    factors = {'condB_coeff': 8.0,
     'L0_ffn_bias': 8.0,
     'L1_cond_W': 6.255,
     'L1_cond_b': 8.0,
     'L1_ffn_A': 5.869,
     'L1_ffn_B': 5.862,
     'L1_ffn_Wr': 6.591}
    for name, (base, spread) in spreads.items():
        noise = np.random.default_rng([zlib.crc32(name.encode()), seed]).standard_normal(out[name].shape)
        drawn = base * np.exp(spread * noise) if base else spread * noise
        out[name] = jnp.asarray(drawn.astype(out[name].dtype))
    for name, factor in factors.items():
        out[name] = (out[name] * factor).astype(out[name].dtype)
    return out
```

```python
from contextlib import ExitStack

import numpy as np

import concourse.bass as bass
from concourse import mybir

F32 = mybir.dt.float32
F32R = mybir.dt.float32r
I32 = mybir.dt.int32
ALU = mybir.AluOpType
ACT = mybir.ActivationFunctionType
AX_X = mybir.AxisListType.X

P = 128
BATCH, SEQ, D = 8, 128, 512
T = BATCH * SEQ
KD = D // P
HALF = T // 2
PAIR = 2 * SEQ
NPAIR = BATCH // 2
F = 1376
FT = -(-F // P)
FPAD = FT * P
RANK = 16
ADAPTERS = 16
LORA_SCALE = 0.5
FFN_SCALE = 2.0
MOE_SCALE = 2.0
EXPERTS = 64
TOPK = 16
JT = EXPERTS * RANK // P
PREP = 4
NEG = -3.0e38
KB = 1024
H_ORDER = [(j + dj, s) for j in range(0, JT, 2) for s in range(2) for dj in range(2)]


def build(nc, x_t, itok, coeff, mask_w, w_gu, w_dn, a_gu, a_dn, b_gu, b_dn,
          lora_a, lora_b, lora_w, w0_t, bias0, w1_t, bias1, wr_t, a_moe, b_moe, consts, out):
    with ExitStack() as ctx:
        base = -(-nc.sbuf_base // 32) * 32
        sems = {}

        def sem(name):
            sems[name] = ctx.enter_context(nc.semaphore(name))
            return sems[name]

        def at(name, shape, dtype, offset):
            return nc.alloc_sbuf_tensor_at(name, shape, dtype, offset=base + offset)

        R_CONST = 0
        R_T = R_CONST + 11 * KB // 4
        R_S = R_T + 8 * KB
        R_WRAW = R_S + 4 * KB
        R_WS = R_WRAW + 8 * KB
        R_BRAW = R_WS + 16 * KB
        R_BS = R_BRAW + 8 * KB
        R_DR = R_BS + 8 * KB
        R_X = R_DR + 11 * KB
        R_AD = R_X + 32 * KB
        R_ACT = R_AD + 22 * KB
        assert base + R_ACT + 88 * KB <= nc.sbuf_usable_end

        const_sb = at("const_sb", [P, 448], F32, R_CONST)
        block_mask = const_sb[:, 0:PAIR]
        ident = const_sb[:, PAIR:PAIR + P]
        ident2 = const_sb[:, PAIR + P:PAIR + P + EXPERTS]
        small = R_CONST + 448 * 4
        bias0_sb = at("bias0_sb", [P, KD], F32, small)
        lora_w_sb = at("lora_w_sb", [P, 1], F32, small + 32)
        coeff_sb = at("coeff_sb", [P, BATCH], F32, small + 64)
        coeff2 = at("coeff2", [P, BATCH], F32, small + 96)
        coeff_neg = at("coeff_neg", [P, BATCH], F32, small + 128)
        itok_sb = at("itok_sb", [1, BATCH], I32, small + 160)
        top8 = at("top8", [P, 4, 2, 8], F32, small + 192)
        gate_sum = at("gate_sum", [P, 4], F32, small + 448)
        gate_inv = at("gate_inv", [P, 4], F32, small + 480)

        x_hl = at("x_hl", [P, 2, KD, T], F32R, R_X)
        w_raw = at("w_raw", [P, 2, 2, KD, P], F32, R_WRAW)
        w_hl = at("w_hl", [P, 2, 2, 2, KD, P], F32R, R_WS)
        b_raw = at("b_raw", [P, 2, 2, NPAIR, P], F32, R_BRAW)
        b_st = at("b_st", [P, 2, 2, NPAIR, P], F32R, R_BS)
        t_st = at("t_st", [P, NPAIR, 2, PAIR], F32R, R_T)
        glu = at("glu", [P, 2, HALF], F32, R_S)
        act = at("act", [P, FT * 2 * T], F32R, R_ACT)
        st = R_ACT + 40 * KB
        x_raw = at("x_raw", [P, KD, T], F32, st)
        a_nat = at("a_nat", [P, 2, D], F32, st + 16 * KB)
        a_st = at("a_st", [P, 2, KD * NPAIR, 4, 32], F32R, st + 20 * KB)
        t_raw = at("t_raw", [P, NPAIR, 2, PAIR], F32, st + 36 * KB)
        ad_nat = at("ad_nat", [P, FPAD], F32, R_DR + FPAD * 4)
        ad_st = at("ad_st", [P, FT * NPAIR, 4, 32], F32R, R_AD)
        wd_raw = at("wd_raw", [P, 2, FT, P], F32, R_DR)
        wd_hl0 = at("wd_hl0", [P, 2, FT, P], F32R, R_X)
        wd_hl1 = at("wd_hl1", [P, 2, FT, P], F32R, R_X + 11 * KB)
        wd_hl = [wd_hl0, wd_hl1]
        bd_st = at("bd_st", [P, 2, NPAIR, P], F32R, R_X + 22 * KB)
        td_st = at("td_st", [P, NPAIR, PAIR], F32R, R_T)
        td_raw = at("td_raw", [P, NPAIR, PAIR], F32, R_S)
        d_hl = at("d_hl", [P, 2, KD, T], F32R, R_WRAW)
        bd_raw = at("bd_raw", [P, NPAIR, D], F32, R_BS)
        la_raw = at("la_raw", [P, D], F32, R_AD)
        la_hl = at("la_hl", [P, 2, D], F32R, R_AD + 2 * KB)
        lb_raw = at("lb_raw", [P, D], F32, R_AD + 6 * KB)
        lb_hl = at("lb_hl", [P, 2, D], F32R, R_AD + 8 * KB)
        w0_raw = at("w0_raw", [P, KD, D], F32, R_AD + 12 * KB)
        w0_hl = at("w0_hl", [P, 2, KD, D], F32R, R_DR)
        x2 = at("x2", [P, KD, T], F32, R_ACT)
        mask_sb = [at("mask_even", [P, KD, D], I32, R_BS), at("mask_odd", [P, KD, D], I32, R_ACT + 80 * KB)]
        w1_raw = at("w1_raw", [P, KD, D], F32, R_AD)
        wc_raw = [at("wc_raw0", [P, KD, D], F32, R_AD + 8 * KB), at("wc_raw1", [P, KD, D], F32, R_X + 8 * KB)]
        wc_hl = at("wc_hl", [P, PREP, 2, KD, D], F32R, R_ACT + 16 * KB)
        bias1_sb = at("bias1_sb", [P, D], F32, R_AD + 16 * KB)
        xs_hl = at("xs_hl", [P, 2, 2, KD, SEQ], F32R, R_T)
        c_tok = at("c_tok", [P, 2, D], F32, R_S)
        c_hl = at("c_hl", [P, 2, KD, T], F32R, R_WRAW)
        wr_raw = at("wr_raw", [P, KD, EXPERTS], F32, R_AD + 18 * KB)
        wr_st = at("wr_st", [P, KD, 2, EXPERTS], F32R, R_AD + 19 * KB)
        s_sb = at("s_sb", [P, HALF], F32, R_DR)
        gate_x = at("gate_x", [P, 2, HALF], F32, R_DR + 2 * KB)
        score = at("score", [P, 4, EXPERTS], F32, R_DR + 6 * KB)
        left1 = at("left1", [P, 4, EXPERTS], F32, R_DR + 7 * KB)
        left2 = at("left2", [P, 4, EXPERTS], F32, R_DR + 8 * KB)
        expo = at("expo", [P, 4, EXPERTS], F32, R_DR + 9 * KB)
        gate2 = at("gate2", [P, 4, 2, EXPERTS], F32, R_DR + 10 * KB)
        am_raw = at("am_raw", [P, 2, KD, P], F32, R_DR + 12 * KB)
        am_hl = at("am_hl", [P, 4, 2, KD, P], F32R, R_X + 16 * KB)
        hg_raw = at("hg_raw", [P, 2, HALF], F32, R_BS)
        hg = at("hg", [P, JT, 2, T], F32R, R_ACT + 16 * KB)
        bm_raw = at("bm_raw", [P, 2, JT, P], F32, R_X + 8 * KB)
        bm_hl = at("bm_hl", [P, 2, 2, JT, P], F32R, R_AD)

        ps = ctx.enter_context(nc.psum_tensor("ps", [P, 8, 512], F32))

        b_sel = nc.dram_tensor("b_sel", (2, P, FPAD), F32).ap()
        bd_sel = nc.dram_tensor("bd_sel", (P, D), F32).ap()

        dma_itok, dma_const, dma_small, dma_x1 = sem("dma_itok"), sem("dma_const"), sem("dma_small"), sem("dma_x1")
        dma_x0 = [sem(f"dma_x0_{k}") for k in range(KD)]
        dma_w = [sem(f"dma_w{u}") for u in range(2)]
        dma_b = [sem(f"dma_b{u}") for u in range(2)]
        dma_a, dma_bsel, dma_ad, dma_bdsel = sem("dma_a"), sem("dma_bsel"), sem("dma_ad"), sem("dma_bdsel")
        dma_wd = [sem(f"dma_wd{u}") for u in range(2)]
        dma_bd, dma_lora, dma_ffn_w = sem("dma_bd"), sem("dma_lora"), sem("dma_ffn_w")
        dma_x2 = [sem(f"dma_x2_{s}") for s in range(2)]
        dma_mask = [sem(f"dma_mask{u}") for u in range(2)]
        dma_cond_w, dma_l1 = sem("dma_cond_w"), sem("dma_l1")
        dma_am = [sem(f"dma_am{u}") for u in range(2)]
        dma_bm = [sem(f"dma_bm{u}") for u in range(2)]
        dma_out = sem("dma_out")
        x_hi, x_lo = sem("x_hi"), sem("x_lo")
        w_hi, w_lo, b_hi, b_lo = sem("w_hi"), sem("w_lo"), sem("b_hi"), sem("b_lo")
        a_tr, a_hi, a_lo = sem("a_tr"), sem("a_hi"), sem("a_lo")
        t_ready, t_masked, t_hi, t_lo = sem("t_ready"), sem("t_masked"), sem("t_hi"), sem("t_lo")
        gate_ready, up_ready = sem("gate_ready"), sem("up_ready")
        silu_done, glu_done, act_hi, act_lo = sem("silu_done"), sem("glu_done"), sem("act_hi"), sem("act_lo")
        ad_tr, ad_hi, ad_lo = sem("ad_tr"), sem("ad_hi"), sem("ad_lo")
        td_ready, td_masked, td_hi, td_lo = sem("td_ready"), sem("td_masked"), sem("td_hi"), sem("td_lo")
        wd_hi, wd_lo, bd_hi, bd_lo = sem("wd_hi"), sem("wd_lo"), sem("bd_hi"), sem("bd_lo")
        d_ready, d_hi, down_banks_free = sem("d_ready"), sem("d_hi"), sem("down_banks_free")
        lb_scaled, lora_hi, lora_lo = sem("lb_scaled"), sem("lora_hi"), sem("lora_lo")
        w0_ready, w0_sum, w0_hi, w0_lo = sem("w0_ready"), sem("w0_sum"), sem("w0_hi"), sem("w0_lo")
        x2_ready, x2_done = sem("x2_ready"), sem("x2_done")
        coeff_done, wc_formed, wc_added = sem("coeff_done"), sem("wc_formed"), sem("wc_added")
        wc_hi, wc_lo, xs_hi, xs_lo = sem("wc_hi"), sem("wc_lo"), sem("xs_hi"), sem("xs_lo")
        c_ready, c_done, ct_ready, ct_hi, ct_lo = sem("c_ready"), sem("c_done"), sem("ct_ready"), sem("ct_hi"), sem("ct_lo")
        wr_hi, wr_lo = sem("wr_hi"), sem("wr_lo")
        s_ready, s_copied, score_ready = sem("s_ready"), sem("s_copied"), sem("score_ready")
        top_step, shifted, exp_done, gate_done = sem("top_step"), sem("shifted"), sem("exp_done"), sem("gate_done")
        gate_tr, late_banks_free = sem("gate_tr"), sem("late_banks_free")
        am_hi, am_lo, h_ready, hg_mul, hg_hi, hg_lo = (sem("am_hi"), sem("am_lo"), sem("h_ready"), sem("hg_mul"),
                                                      sem("hg_hi"), sem("hg_lo"))
        bm_hi, bm_lo, o_ready = sem("bm_hi"), sem("bm_lo"), sem("o_ready")

        def rows3(v):
            return v.unsqueeze(2).broadcast_to([P, v.shape[1], 3, 32])

        block = ctx.enter_context(nc.Block())

        @block.sync
        def _(sp):
            sp.dma_start(itok_sb[:], itok).then_inc(dma_itok, 16)

            def load_x0(k):
                sp.dma_start(x_raw[:, k, 0:HALF], x_t[:, k, 0:HALF]).then_inc(dma_x0[k], 16)

            load_x0(0)
            sp.dma_start(w_raw[:, 0], w_gu[0]).then_inc(dma_w[0], 16)
            for k in range(1, KD):
                load_x0(k)
            sp.dma_start(x_raw[:, :, HALF:T], x_t[:, :, HALF:T]).then_inc(dma_x1, 16)
            sp.dma_start(const_sb[:], consts).then_inc(dma_const, 16)
            sp.dma_start(w_raw[:, 1], w_gu[1]).then_inc(dma_w[1], 16)

            def load_b(cols, slot):
                for q in range(4):
                    src = b_sel.rearrange("m (p r) f -> r (m p) f", p=NPAIR)[:, :, cols]
                    dst = b_raw[32 * q:32 * q + 32, slot].rearrange("r m p f -> r (m p) f")
                    sp.dma_start(dst, src).then_inc(dma_b[slot], 16)

            sp.wait_ge(dma_bsel, 16 * BATCH)
            for f in range(2):
                load_b(slice(f * P, f * P + P), f)
            sp.dma_start(bias0_sb[:], bias0).then_inc(dma_small, 16)
            sp.dma_start(lora_w_sb[:], lora_w).then_inc(dma_small, 16)
            sp.dma_start(coeff_sb[:], coeff.partition_broadcast(P)).then_inc(dma_small, 16)
            sp.dma_start(wd_raw[:, 0], w_dn[0]).then_inc(dma_wd[0], 16)

            def load_tile(f, slot):
                for made in (w_hi, w_lo):
                    sp.wait_ge(made, f - 1)
                sp.dma_start(w_raw[:, slot], w_gu[bass.ds(f, 1)]).then_inc(dma_w[slot], 16)
                for made in (b_hi, b_lo):
                    sp.wait_ge(made, f - 1)
                load_b(bass.ds(f * P, P), slot)

            with sp.Fori(0, (FT - 3) // 2) as i:
                for u in range(2):
                    load_tile(2 * i + 2 + u, u)
            load_tile(FT - 1, 0)

            sp.wait_ge(ad_tr, FT)
            sp.dma_start(wd_raw[:, 1], w_dn[1]).then_inc(dma_wd[1], 16)
            sp.wait_ge(up_ready, 2 * FT)
            sp.wait_ge(dma_bdsel, 16 * BATCH)
            for q in range(4):
                sp.dma_start(bd_raw[32 * q:32 * q + 32], bd_sel.rearrange("(p r) o -> r p o", p=NPAIR)).then_inc(dma_bd, 16)
            sp.wait_ge(td_ready, NPAIR)
            sp.dma_start(la_raw[:], lora_a).then_inc(dma_lora, 16)
            sp.dma_start(lb_raw[:], lora_b).then_inc(dma_lora, 16)
            sp.dma_start(w0_raw[:], w0_t).then_inc(dma_ffn_w, 16)
            for o in (2, 3):
                sp.wait_ge(wd_hi, o - 1)
                sp.wait_ge(wd_lo, o - 1)
                sp.dma_start(wd_raw[:, o % 2], w_dn[o]).then_inc(dma_wd[o % 2], 16)

            def load_mask(b):
                if b >= 2:
                    sp.wait_ge(wc_formed, b - 1)
                sp.dma_start(mask_sb[b % 2][:], mask_w[b]).then_inc(dma_mask[b % 2], 16)

            sp.wait_ge(bd_hi, KD)
            sp.wait_ge(bd_lo, KD)
            load_mask(0)
            sp.wait_ge(w0_hi, KD)
            sp.wait_ge(w0_lo, KD)
            sp.dma_start(w1_raw[:], w1_t).then_inc(dma_cond_w, 16)
            sp.dma_start(bias1_sb[:], bias1.partition_broadcast(P)).then_inc(dma_l1, 16)
            sp.dma_start(wr_raw[:], wr_t).then_inc(dma_l1, 16)
            sp.wait_ge(d_ready, 2 * KD)
            load_mask(1)
            for s in range(2):
                half = slice(s * HALF, s * HALF + HALF)
                sp.dma_start(x2[:, :, half], x_t[:, :, half]).then_inc(dma_x2[s], 16)
                load_mask(2 + s)
            load_mask(4)
            load_mask(5)

            def load_am(j):
                if j >= 2:
                    sp.wait_ge(am_hi, j - 1)
                    sp.wait_ge(am_lo, j - 1)
                sp.dma_start(am_raw[:, j % 2], a_moe[j]).then_inc(dma_am[j % 2], 16)

            sp.wait_ge(x2_ready, 2 * KD)
            load_am(0)
            load_am(1)
            load_mask(6)
            load_mask(7)
            for j in range(2, 4):
                load_am(j)
            sp.wait_ge(wc_hi, BATCH)
            sp.wait_ge(wc_lo, BATCH)
            for o in range(2):
                sp.dma_start(bm_raw[:, o], b_moe[o]).then_inc(dma_bm[o], 16)
            for j in range(4, JT):
                load_am(j)
            for o in range(2, KD):
                sp.wait_ge(bm_hi, o - 1)
                sp.wait_ge(bm_lo, o - 1)
                sp.dma_start(bm_raw[:, o % 2], b_moe[o]).then_inc(dma_bm[o % 2], 16)
            for n in range(2 * KD):
                o, s = n // 2, n % 2
                sp.wait_ge(late_banks_free, 4 + n + 1)
                half = slice(s * HALF, s * HALF + HALF)
                sp.dma_start(out[o, :, half], x2[:, o, half]).then_inc(dma_out, 16)
            sp.wait_ge(dma_out, 16 * 2 * KD)

        @block.gpsimd
        def _(pool):
            pool.wait_ge(dma_itok, 16)
            adapter = [pool.value_load(itok_sb[0:1, b:b + 1], min_val=0, max_val=ADAPTERS - 1) for b in range(BATCH)]

            def mine(b):
                return slice(RANK * b, RANK * b + RANK)

            for b in range(BATCH):
                pool.dma_start(a_nat[mine(b)], a_gu[bass.ds(adapter[b], 1)]).then_inc(dma_a, 16)
            for b in range(BATCH):
                pool.dma_start(b_sel[:, mine(b)], b_gu[bass.ds(adapter[b], 1)]).then_inc(dma_bsel, 16)
            for b in range(BATCH):
                pool.dma_start(ad_nat[mine(b)], a_dn[bass.ds(adapter[b], 1)]).then_inc(dma_ad, 16)
            for b in range(BATCH):
                pool.dma_start(bd_sel[mine(b)], b_dn[bass.ds(adapter[b], 1)]).then_inc(dma_bdsel, 16)
            pool.wait_ge(dma_cond_w, 16)
            for b in range(BATCH):
                pool.wait_ge(wc_formed, b + 1)
                wc = wc_raw[b % 2]
                nc.gpsimd.tensor_tensor(wc[:], wc[:], w1_raw[:], ALU.add).then_inc(wc_added, 1)

            def am_low(j):
                pool.wait_ge(am_hi, j + 1)
                nc.gpsimd.tensor_tensor(am_hl[:, j % 4, 1], am_raw[:, j % 2], am_hl[:, j % 4, 0].bitcast(F32),
                                        ALU.subtract).then_inc(am_lo, 1)

            def bm_low(o):
                pool.wait_ge(bm_hi, o + 1)
                nc.gpsimd.tensor_tensor(bm_hl[:, o % 2, 1], bm_raw[:, o % 2], bm_hl[:, o % 2, 0].bitcast(F32),
                                        ALU.subtract).then_inc(bm_lo, 1)

            for j in range(JT):
                am_low(j)
            for o in range(KD):
                bm_low(o)

        @block.scalar
        def _(act_e):
            def copy(out, in_):
                return nc.scalar.activation(out, in_, ACT.Copy)

            def x_high(k, s):
                if s == 0:
                    act_e.wait_ge(dma_x0[k], 16)
                else:
                    act_e.wait_ge(dma_x1, 16)
                half = slice(s * HALF, s * HALF + HALF)
                copy(x_hl[:, 0, k, half], x_raw[:, k, half]).then_inc(x_hi, 1)

            def split(f, slot, use):
                act_e.wait_ge(dma_w[slot], 16 * use)
                if not isinstance(f, int) or f >= 2:
                    act_e.wait_ge(up_ready, 2 * f - 2)
                copy(w_hl[:, slot, 0], w_raw[:, slot]).then_inc(w_hi, 1)
                act_e.wait_ge(dma_b[slot], 64 * use)
                copy(b_st[:, slot], b_raw[:, slot]).then_inc(b_hi, 1)

            def evacuate(f, first=False):
                for s in range(2):
                    act_e.wait_ge(gate_ready, 2 * f + s + 1)
                    if not first:
                        act_e.wait_ge(act_lo, 2 * f + s - 1)
                    nc.scalar.activation(glu[:, s], ps[:, 2 * s], ACT.Silu).then_inc(silu_done, 1)
                    act_e.wait_ge(glu_done, 2 * f + s + 1)
                    copy(act[:, bass.ds(f * (2 * T) + s * HALF, HALF)], glu[:, s]).then_inc(act_hi, 1)

            x_high(0, 0)
            act_e.wait_ge(dma_w[0], 16)
            copy(w_hl[:, 0, 0], w_raw[:, 0]).then_inc(w_hi, 1)
            for k in range(1, KD):
                x_high(k, 0)
            for k in range(KD):
                x_high(k, 1)
            for m in range(2):
                act_e.wait_ge(a_tr, KD * (m + 1))
                copy(a_st[:, m, :, 0:3, :], rows3(ps[:, 4 + m].rearrange("p (n c) -> p n c", c=32))).then_inc(a_hi, 1)
            act_e.wait_ge(dma_b[0], 64)
            copy(b_st[:, 0], b_raw[:, 0]).then_inc(b_hi, 1)
            for p in range(NPAIR):
                act_e.wait_ge(t_masked, p + 1)
                copy(t_st[:, p], t_raw[:, p]).then_inc(t_hi, 1)
            split(1, 1, 1)
            evacuate(0, first=True)
            for g in range(3):
                n = min(4, FT - 4 * g)
                act_e.wait_ge(ad_tr, 4 * g + n)
                copy(ad_st[:, 16 * g:16 * g + 4 * n, 0:3, :],
                     rows3(ps[:, 4 + g, 0:n * P].rearrange("p (n c) -> p n c", c=32))).then_inc(ad_hi, 1)
            with act_e.Fori(0, (FT - 3) // 2) as i:
                for u in range(2):
                    split(2 * i + 2 + u, u, i + 2)
                    evacuate(2 * i + 1 + u)
            split(FT - 1, 0, (FT - 1) // 2 + 1)
            evacuate(FT - 2)
            evacuate(FT - 1)

            def wd_high(o):
                act_e.wait_ge(dma_wd[o % 2], 16 * (o // 2 + 1))
                if o < 2:
                    act_e.wait_ge(up_ready, 2 * FT)
                else:
                    act_e.wait_ge(d_ready, 2 * o - 2)
                copy(wd_hl[o % 2][:, 0], wd_raw[:, o % 2]).then_inc(wd_hi, 1)

            def bd_high(o):
                act_e.wait_ge(dma_bd, 64)
                copy(bd_st[:, o % 2], bd_raw[:, :, o * P:o * P + P]).then_inc(bd_hi, 1)

            def d_high(o):
                for s in range(2):
                    act_e.wait_ge(d_ready, 2 * o + s + 1)
                    copy(d_hl[:, 0, o, s * HALF:s * HALF + HALF], ps[:, 2 * (o % 2) + s]).then_inc(d_hi, 1)

            wd_high(0)
            for p in range(NPAIR):
                act_e.wait_ge(td_masked, p + 1)
                copy(td_st[:, p], td_raw[:, p]).then_inc(td_hi, 1)
            bd_high(0)
            wd_high(1)
            bd_high(1)
            act_e.wait_ge(dma_lora, 32)
            copy(la_hl[:, 0], la_raw[:]).then_inc(lora_hi, 1)
            act_e.wait_ge(lb_scaled, 1)
            copy(lb_hl[:, 0], lb_raw[:]).then_inc(lora_hi, 1)
            for o in range(KD):
                d_high(o)
                if o + 2 < KD:
                    wd_high(o + 2)
                    bd_high(o + 2)
                if o == 2:
                    for k in range(KD):
                        act_e.wait_ge(w0_sum, k + 1)
                        copy(w0_hl[:, 0, k], w0_raw[:, k]).then_inc(w0_hi, 1)

            def form(b):
                act_e.wait_ge(dma_mask[b % 2], 16 * (b // 2 + 1))
                if b == 0:
                    act_e.wait_ge(coeff_done, 2)
                    act_e.wait_ge(w0_lo, KD)
                    act_e.wait_ge(w0_hi, KD)
                elif b == 1:
                    act_e.wait_ge(d_ready, 2 * KD)
                else:
                    act_e.wait_ge(wc_lo, b - 1)
                    act_e.wait_ge(wc_hi, b - 1)
                nc.scalar.activation(wc_raw[b % 2][:], mask_sb[b % 2][:], ACT.Identity, bias=coeff_neg[:, b:b + 1],
                                     scale=coeff2[:, b:b + 1]).then_inc(wc_formed, 1)

            def wc_high(b):
                act_e.wait_ge(wc_added, b + 1)
                if b == 0:
                    act_e.wait_ge(d_ready, 2 * KD)
                if b >= PREP:
                    act_e.wait_ge(c_ready, b - PREP + 1)
                copy(wc_hl[:, b % PREP, 0], wc_raw[b % 2][:]).then_inc(wc_hi, 1)

            def xs_high(b):
                act_e.wait_ge(x2_done, KD if b < BATCH // 2 else 2 * KD)
                if b >= 2:
                    act_e.wait_ge(c_ready, b - 1)
                copy(xs_hl[:, b % 2, 0], x2[:, :, b * SEQ:b * SEQ + SEQ]).then_inc(xs_hi, 1)

            def am_high(j):
                act_e.wait_ge(dma_am[j % 2], 16 * (j // 2 + 1))
                if j >= 4:
                    act_e.wait_ge(h_ready, H_ORDER.index((j - 4, 1)) + 1)
                copy(am_hl[:, j % 4, 0], am_raw[:, j % 2]).then_inc(am_hi, 1)

            def s_copy(s):
                act_e.wait_ge(s_ready, s + 1)
                copy(s_sb[:], ps[:, 4]).then_inc(s_copied, 1)

            def exponent(s):
                act_e.wait_ge(shifted, s + 1)
                nc.scalar.activation(expo[:], expo[:], ACT.Exp).then_inc(exp_done, 1)

            def gate_copy(s):
                act_e.wait_ge(gate_tr, s + 1)
                copy(gate_x[:, s], ps[:, 6]).then_inc(late_banks_free, 2)

            form(0)
            form(1)
            wc_high(0)
            act_e.wait_ge(dma_l1, 32)
            copy(wr_st[:, :, 0], wr_raw[:]).then_inc(wr_hi, 1)
            form(2)
            wc_high(1)
            xs_high(0)
            for b in range(BATCH):
                if b + 1 < BATCH:
                    xs_high(b + 1)
                if b + 3 < BATCH:
                    form(b + 3)
                if b + 2 < BATCH:
                    wc_high(b + 2)
                if b == 6:
                    s_copy(0)
                    exponent(0)
                if b in (3, 4, 5, 6):
                    am_high(b - 3)
                act_e.wait_ge(ct_ready, b + 1)
                copy(c_hl[:, 0, :, b * SEQ:b * SEQ + SEQ],
                     ps[:, 2 + b % 2].rearrange("p (o t) -> p o t", t=SEQ)).then_inc(ct_hi, 1)

            def hg_high(n):
                j, s = H_ORDER[n]
                act_e.wait_ge(hg_mul, n + 1)
                copy(hg[:, j, 0, s * HALF:s * HALF + HALF], hg_raw[:, n % 2]).then_inc(hg_hi, 1)

            def bm_high(o):
                act_e.wait_ge(dma_bm[o % 2], 16 * (o // 2 + 1))
                if o >= 2:
                    act_e.wait_ge(o_ready, 2 * o - 2)
                copy(bm_hl[:, o % 2, 0], bm_raw[:, o % 2]).then_inc(bm_hi, 1)

            gate_copy(0)
            hg_high(0)
            hg_high(1)
            s_copy(1)
            exponent(1)
            gate_copy(1)
            for n in range(2, 2 * JT):
                hg_high(n)
                if n % 4 == 3 and n // 4 < 2:
                    am_high(n // 2 + 3)
                    am_high(n // 2 + 4)
                if n in (8, 10):
                    bm_high((n - 8) // 2)
            for o in range(2, KD):
                bm_high(o)

        @block.vector
        def _(dve):
            def low(out, whole, high):
                return nc.vector.tensor_tensor(out, whole, high.bitcast(F32), ALU.subtract)

            def x_low(k, s):
                n = KD * s + k
                dve.wait_ge(x_hi, n + 1)
                half = slice(s * HALF, s * HALF + HALF)
                low(x_hl[:, 1, k, half], x_raw[:, k, half], x_hl[:, 0, k, half]).then_inc(x_lo, 1)

            def w_low(f, slot):
                dve.wait_ge(w_hi, f + 1)
                low(w_hl[:, slot, 1], w_raw[:, slot], w_hl[:, slot, 0]).then_inc(w_lo, 1)

            def b_low(f, slot):
                dve.wait_ge(b_hi, f + 1)
                low(b_st[64:96, slot], b_raw[64:96, slot], b_st[64:96, slot]).then_inc(b_lo, 1)

            def evacuate(f):
                for s in range(2):
                    dve.wait_ge(silu_done, 2 * f + s + 1)
                    dve.wait_ge(up_ready, 2 * f + s + 1)
                    done = nc.vector.tensor_tensor(glu[:, s], glu[:, s], ps[:, 2 * s + 1], ALU.mult)
                    done.then_inc(glu_done, 1)
                    dve.wait_ge(act_hi, 2 * f + s + 1)
                    low(act[:, bass.ds(f * (2 * T) + T + s * HALF, HALF)], glu[:, s],
                        act[:, bass.ds(f * (2 * T) + s * HALF, HALF)]).then_inc(act_lo, 1)

            x_low(0, 0)
            w_low(0, 0)
            for k in range(1, KD):
                x_low(k, 0)
            for k in range(KD):
                x_low(k, 1)
            for m in range(2):
                dve.wait_ge(a_hi, m + 1)
                low(a_st[:, m, :, 3, :], ps[:, 4 + m].rearrange("p (n c) -> p n c", c=32),
                    a_st[:, m, :, 0, :]).then_inc(a_lo, 1)
            b_low(0, 0)
            dve.wait_ge(dma_const, 16)
            mask2 = block_mask.unsqueeze(1).broadcast_to([P, 2, PAIR])

            def t_mask(p):
                dve.wait_ge(t_ready, p + 1)
                nc.vector.tensor_tensor(t_raw[:, p], ps[:, 4 + p].rearrange("p (m t) -> p m t", m=2), mask2,
                                        ALU.mult).then_inc(t_masked, 1)

            def t_low(p):
                dve.wait_ge(t_hi, p + 1)
                low(t_st[32:64, p], t_raw[32:64, p], t_st[32:64, p]).then_inc(t_lo, 1)

            for p in range(NPAIR):
                t_mask(p)
                if p:
                    t_low(p - 1)
            t_low(NPAIR - 1)
            w_low(1, 1)
            b_low(1, 1)
            evacuate(0)
            for g in range(3):
                n = min(4, FT - 4 * g)
                dve.wait_ge(ad_hi, g + 1)
                low(ad_st[:, 16 * g:16 * g + 4 * n, 3, :], ps[:, 4 + g, 0:n * P].rearrange("p (n c) -> p n c", c=32),
                    ad_st[:, 16 * g:16 * g + 4 * n, 0, :]).then_inc(ad_lo, 1)
            with dve.Fori(0, (FT - 3) // 2) as i:
                for u in range(2):
                    w_low(2 * i + 2 + u, u)
                    b_low(2 * i + 2 + u, u)
                    evacuate(2 * i + 1 + u)
            w_low(FT - 1, 0)
            b_low(FT - 1, 0)
            evacuate(FT - 2)
            f = FT - 1
            for s in range(2):
                dve.wait_ge(silu_done, 2 * f + s + 1)
                dve.wait_ge(up_ready, 2 * f + s + 1)
                nc.vector.tensor_tensor(glu[:, s], glu[:, s], ps[:, 2 * s + 1], ALU.mult).then_inc(glu_done, 1)
                dve.wait_ge(act_hi, 2 * f + s + 1)
                low(act[:, f * 2 * T + T + s * HALF:f * 2 * T + T + s * HALF + HALF], glu[:, s],
                    act[:, f * 2 * T + s * HALF:f * 2 * T + s * HALF + HALF]).then_inc(act_lo, 1)

            def wd_low(o):
                dve.wait_ge(wd_hi, o + 1)
                low(wd_hl[o % 2][:, 1], wd_raw[:, o % 2], wd_hl[o % 2][:, 0]).then_inc(wd_lo, 1)

            def bd_low(o):
                dve.wait_ge(bd_hi, o + 1)
                low(bd_st[64:96, o % 2], bd_raw[64:96, :, o * P:o * P + P], bd_st[64:96, o % 2]).then_inc(bd_lo, 1)

            def d_low(o):
                for s in range(2):
                    half = slice(s * HALF, s * HALF + HALF)
                    dve.wait_ge(d_hi, 2 * o + s + 1)
                    low(d_hl[:, 1, o, half], ps[:, 2 * (o % 2) + s], d_hl[:, 0, o, half]).then_inc(down_banks_free, 1)

            wd_low(0)
            for p in range(NPAIR):
                dve.wait_ge(td_ready, p + 1)
                dve.wait_ge(act_lo, 2 * FT)
                nc.vector.tensor_tensor(td_raw[:, p], ps[:, 4 + p, 0:PAIR], block_mask, ALU.mult).then_inc(td_masked, 1)
                dve.wait_ge(td_hi, p + 1)
                low(td_st[32:64, p], td_raw[32:64, p], td_st[32:64, p]).then_inc(td_lo, 1)
            bd_low(0)
            wd_low(1)
            bd_low(1)
            dve.wait_ge(dma_small, 48)
            nc.vector.tensor_scalar(coeff2[:], coeff_sb[:], 2.0, None, ALU.mult).then_inc(coeff_done, 1)
            nc.vector.tensor_scalar(coeff_neg[:], coeff_sb[:], -1.0, None, ALU.mult).then_inc(coeff_done, 1)
            dve.wait_ge(dma_lora, 32)
            nc.vector.tensor_scalar(lb_raw[:], lb_raw[:], lora_w_sb[:, 0:1], FFN_SCALE, ALU.mult,
                                    ALU.mult).then_inc(lb_scaled, 1)
            dve.wait_ge(lora_hi, 1)
            low(la_hl[:, 1], la_raw[:], la_hl[:, 0]).then_inc(lora_lo, 1)
            dve.wait_ge(lora_hi, 2)
            low(lb_hl[:, 1], lb_raw[:], lb_hl[:, 0]).then_inc(lora_lo, 1)
            for o in range(KD):
                d_low(o)
                if o + 2 < KD:
                    wd_low(o + 2)
                    bd_low(o + 2)
                if o == 2:
                    dve.wait_ge(dma_ffn_w, 16)
                    for k in range(KD):
                        dve.wait_ge(w0_ready, k + 1)
                        nc.vector.tensor_tensor(w0_raw[:, k], w0_raw[:, k], ps[:, 4 + k], ALU.add).then_inc(w0_sum, 1)
                    for k in range(KD):
                        dve.wait_ge(w0_hi, k + 1)
                        low(w0_hl[:, 1, k], w0_raw[:, k], w0_hl[:, 0, k]).then_inc(w0_lo, 1)

            def x2_add(s):
                dve.wait_ge(dma_x2[s], 16)
                for o in range(KD):
                    half = slice(s * HALF, s * HALF + HALF)
                    dve.wait_ge(x2_ready, KD * s + o + 1)
                    nc.vector.scalar_tensor_tensor(x2[:, o, half], ps[:, 4 * (1 - s) + o], bias0_sb[:, o:o + 1],
                                                   x2[:, o, half], ALU.add, ALU.add).then_inc(x2_done, 1)

            def wc_low(b):
                dve.wait_ge(wc_hi, b + 1)
                low(wc_hl[:, b % PREP, 1], wc_raw[b % 2][:], wc_hl[:, b % PREP, 0]).then_inc(wc_lo, 1)

            def xs_low(b):
                dve.wait_ge(xs_hi, b + 1)
                low(xs_hl[:, b % 2, 1], x2[:, :, b * SEQ:b * SEQ + SEQ], xs_hl[:, b % 2, 0]).then_inc(xs_lo, 1)

            def c_bias(b):
                dve.wait_ge(c_ready, b + 1)
                if b >= 2:
                    dve.wait_ge(ct_ready, b - 1)
                nc.vector.tensor_tensor(c_tok[:, b % 2], ps[:, b % 2], bias1_sb[:], ALU.add).then_inc(c_done, 1)

            def ct_low(b):
                dve.wait_ge(ct_hi, b + 1)
                cols = slice(b * SEQ, b * SEQ + SEQ)
                low(c_hl[:, 1, :, cols], ps[:, 2 + b % 2].rearrange("p (o t) -> p o t", t=SEQ),
                    c_hl[:, 0, :, cols]).then_inc(ct_lo, 1)

            steps = [0]

            def step(ins):
                steps[0] += 1
                ins.then_inc(top_step, 1)
                dve.wait_ge(top_step, steps[0])

            def route(s):
                dve.wait_ge(score_ready, s + 1)
                step(nc.vector.tensor_copy(score[:], ps[:, 5, 0:4 * EXPERTS].rearrange("p (t e) -> p t e", t=4)))
                for t in range(4):
                    last = nc.vector.max(top8[:, t, 0], score[:, t])
                step(last)
                nc.vector.tensor_tensor(expo[:], score[:], top8[:, :, 0, 0:1].broadcast_to([P, 4, EXPERTS]),
                                        ALU.subtract).then_inc(shifted, 1)
                for t in range(4):
                    last = nc.vector.match_replace(left1[:, t], top8[:, t, 0], score[:, t], NEG)
                step(last)
                for t in range(4):
                    last = nc.vector.max(top8[:, t, 1], left1[:, t])
                step(last)
                for t in range(4):
                    last = nc.vector.match_replace(left2[:, t], top8[:, t, 1], left1[:, t], NEG)
                step(last)
                step(nc.vector.tensor_tensor(left2[:], left2[:], score[:], ALU.not_equal))
                dve.wait_ge(exp_done, s + 1)
                step(nc.vector.tensor_tensor(left1[:], expo[:], left2[:], ALU.mult))
                step(nc.vector.tensor_reduce(gate_sum[:], left1[:], AX_X, ALU.add))
                step(nc.vector.reciprocal(gate_inv[:], gate_sum[:]))
                if s:
                    dve.wait_ge(gate_tr, s)
                for t in range(4):
                    last = nc.vector.tensor_scalar(
                        gate2[:, t], left1[:, t].unsqueeze(1).broadcast_to([P, 2, EXPERTS]),
                        gate_inv[:, t:t + 1], MOE_SCALE, ALU.mult, ALU.mult)
                last.then_inc(gate_done, 1)

            x2_add(0)
            wc_low(0)
            dve.wait_ge(wr_hi, 1)
            low(wr_st[:, :, 1], wr_raw[:], wr_st[:, :, 0]).then_inc(wr_lo, 1)
            x2_add(1)
            xs_low(0)
            wc_low(1)
            dve.wait_ge(dma_l1, 32)
            for b in range(BATCH):
                c_bias(b)
                if b + 1 < BATCH:
                    xs_low(b + 1)
                if b + 2 < BATCH:
                    wc_low(b + 2)
                if b == 6:
                    route(0)
                ct_low(b)

            def hg_gate(n):
                j, s = H_ORDER[n]
                dve.wait_ge(h_ready, n + 1)
                dve.wait_ge(late_banks_free, 2 * (s + 1))
                if n >= 2:
                    dve.wait_ge(hg_hi, n - 1)
                    dve.wait_ge(hg_lo, n - 1)
                nc.vector.tensor_tensor(hg_raw[:, n % 2], ps[:, 2 * (j % 2) + s], gate_x[:, s],
                                        ALU.mult).then_inc(hg_mul, 1)

            def hg_low(n):
                j, s = H_ORDER[n]
                half = slice(s * HALF, s * HALF + HALF)
                dve.wait_ge(hg_hi, n + 1)
                low(hg[:, j, 1, half], hg_raw[:, n % 2], hg[:, j, 0, half]).then_inc(hg_lo, 1)

            hg_gate(0)
            hg_gate(1)
            hg_low(0)
            hg_low(1)
            route(1)
            for n in range(2, 2 * JT):
                hg_gate(n)
                if n >= 3:
                    hg_low(n - 1)
            hg_low(2 * JT - 1)
            for n in range(2 * KD):
                o, s = n // 2, n % 2
                half = slice(s * HALF, s * HALF + HALF)
                dve.wait_ge(o_ready, n + 1)
                nc.vector.tensor_tensor(x2[:, o, half], ps[:, 4 + n % 4], x2[:, o, half], ALU.add)\
                    .then_inc(late_banks_free, 1)

        @block.tensor
        def _(pe):
            def mm3(out, w_high, w_low, m_high, m_low, start, stop):
                nc.tensor.matmul(out, w_high, m_high, start=start, stop=False)
                nc.tensor.matmul(out, w_high, m_low, start=False, stop=False)
                return nc.tensor.matmul(out, w_low, m_high, start=False, stop=stop)

            def halves(s):
                return slice(s * HALF, s * HALF + HALF)

            def project(slot, m, s, wait_x=False):
                for k in range(KD):
                    if wait_x:
                        pe.wait_ge(x_hi, KD * s + k + 1)
                        pe.wait_ge(x_lo, KD * s + k + 1)
                    mm3(ps[:, 2 * s + m], w_hl[:, slot, 0, m, k], w_hl[:, slot, 1, m, k],
                        x_hl[:, 0, k, halves(s)], x_hl[:, 1, k, halves(s)], k == 0, False)

            def adapt(slot, m, s):
                for h in range(2):
                    last = nc.tensor.matmul(ps[:, 2 * s + m, h * PAIR:h * PAIR + PAIR], b_st[:, slot, m, 2 * s + h],
                                            t_st[:, 2 * s + h, m], start=False, stop=h == 1)
                last.then_inc(up_ready if m else gate_ready, 1)

            pe.wait_ge(w_hi, 1)
            pe.wait_ge(w_lo, 1)
            project(0, 0, 0, wait_x=True)
            project(0, 1, 0)
            pe.wait_ge(dma_a, 16 * BATCH)
            pe.wait_ge(dma_const, 16)
            for m in range(2):
                for k in range(KD):
                    nc.tensor.transpose(ps[:, 4 + m, k * P:k * P + P], a_nat[:, m, k * P:k * P + P],
                                        ident).then_inc(a_tr, 1)
            project(0, 0, 1, wait_x=True)
            project(0, 1, 1)
            pe.wait_ge(a_hi, 2)
            pe.wait_ge(a_lo, 2)
            for p in range(NPAIR):
                cols = slice(p * PAIR, p * PAIR + PAIR)
                for m in range(2):
                    for k in range(KD):
                        stack = a_st[:, m, NPAIR * k + p].rearrange("p c r -> p (c r)")
                        for h in range(2):
                            last = nc.tensor.matmul(ps[:, 4 + p, m * PAIR:m * PAIR + PAIR], stack,
                                                    x_hl[:, h, k, cols], start=(k == 0 and h == 0),
                                                    stop=(k == KD - 1 and h == 1))
                last.then_inc(t_ready, 1)
            pe.wait_ge(b_hi, 1)
            pe.wait_ge(b_lo, 1)
            for s in range(2):
                pe.wait_ge(t_hi, 2 * s + 2)
                pe.wait_ge(t_lo, 2 * s + 2)
                for m in range(2):
                    adapt(0, m, s)
            pe.wait_ge(dma_ad, 16 * BATCH)
            for f in range(FT):
                nc.tensor.transpose(ps[:, 4 + f // 4, (f % 4) * P:(f % 4) * P + P], ad_nat[:, f * P:f * P + P],
                                    ident).then_inc(ad_tr, 1)
            with pe.Fori(0, (FT - 1) // 2) as i:
                for u in range(2):
                    f, slot = 2 * i + 1 + u, (u + 1) % 2
                    pe.wait_ge(w_hi, f + 1)
                    pe.wait_ge(w_lo, f + 1)
                    for s in range(2):
                        pe.wait_ge(silu_done, 2 * f + s - 1)
                        project(slot, 0, s)
                        if s == 0:
                            pe.wait_ge(b_hi, f + 1)
                            pe.wait_ge(b_lo, f + 1)
                        adapt(slot, 0, s)
                        pe.wait_ge(glu_done, 2 * f + s - 1)
                        project(slot, 1, s)
                        adapt(slot, 1, s)

            def act_part(f, h, lo, n):
                at0 = f * 2 * T + h * T + lo
                return act[:, at0:at0 + n]

            pe.wait_ge(ad_hi, 3)
            pe.wait_ge(ad_lo, 3)
            for f in range(FT):
                for p in range(NPAIR):
                    if p % 2 == 0:
                        pe.wait_ge(act_hi, 2 * f + p // 2 + 1)
                        pe.wait_ge(act_lo, 2 * f + p // 2 + 1)
                    stack = ad_st[:, NPAIR * f + p].rearrange("p c r -> p (c r)")
                    for h in range(2):
                        last = nc.tensor.matmul(ps[:, 4 + p, 0:PAIR], stack, act_part(f, h, p * PAIR, PAIR),
                                                start=(f == 0 and h == 0), stop=(f == FT - 1 and h == 1))
                    if f == FT - 1:
                        last.then_inc(td_ready, 1)

            def down(o, u):
                pe.wait_ge(wd_hi, o + 1)
                pe.wait_ge(wd_lo, o + 1)
                for s in range(2):
                    if not isinstance(o, int) or o >= 2:
                        pe.wait_ge(down_banks_free, 2 * o + s - 3)
                    for f in range(FT):
                        mm3(ps[:, 2 * u + s], wd_hl[u][:, 0, f], wd_hl[u][:, 1, f],
                            act_part(f, 0, s * HALF, HALF), act_part(f, 1, s * HALF, HALF), f == 0, False)
                    pe.wait_ge(bd_hi, o + 1)
                    pe.wait_ge(bd_lo, o + 1)
                    pe.wait_ge(td_hi, 2 * s + 2)
                    pe.wait_ge(td_lo, 2 * s + 2)
                    for h in range(2):
                        last = nc.tensor.matmul(ps[:, 2 * u + s, h * PAIR:h * PAIR + PAIR], bd_st[:, u, 2 * s + h],
                                                td_st[:, 2 * s + h], start=False, stop=h == 1)
                    last.then_inc(d_ready, 1)

            pe.wait_ge(glu_done, 2 * FT)
            down(0, 0)
            down(1, 1)
            down(2, 0)
            pe.wait_ge(lora_hi, 2)
            pe.wait_ge(lora_lo, 2)
            pe.wait_ge(td_masked, NPAIR)
            for k in range(KD):
                cols = slice(k * P, k * P + P)
                mm3(ps[:, 4 + k], la_hl[:, 0, cols], la_hl[:, 1, cols], lb_hl[:, 0], lb_hl[:, 1], True,
                    True).then_inc(w0_ready, 1)
            down(3, 1)

            pe.wait_ge(w0_hi, KD)
            pe.wait_ge(w0_lo, KD)
            for s in range(2):
                pe.wait_ge(down_banks_free, 2 * KD - 1 + s)
                for o in range(KD):
                    cols = slice(o * P, o * P + P)
                    for k in range(KD):
                        last = mm3(ps[:, 4 * (1 - s) + o], w0_hl[:, 0, k, cols], w0_hl[:, 1, k, cols],
                                   d_hl[:, 0, k, halves(s)], d_hl[:, 1, k, halves(s)], k == 0, k == KD - 1)
                    last.then_inc(x2_ready, 1)

            def cond(b):
                pe.wait_ge(xs_hi, b + 1)
                pe.wait_ge(xs_lo, b + 1)
                pe.wait_ge(wc_hi, b + 1)
                pe.wait_ge(wc_lo, b + 1)
                if b < 2:
                    pe.wait_ge(x2_done, KD + 1 + b)
                else:
                    pe.wait_ge(c_done, b - 1)
                for k in range(KD):
                    last = mm3(ps[:, b % 2], xs_hl[:, b % 2, 0, k], xs_hl[:, b % 2, 1, k],
                               wc_hl[:, b % PREP, 0, k], wc_hl[:, b % PREP, 1, k], k == 0, k == KD - 1)
                last.then_inc(c_ready, 1)

            def turn(b):
                pe.wait_ge(c_done, b + 1)
                if b < 2:
                    pe.wait_ge(x2_done, KD + 3 + b)
                else:
                    pe.wait_ge(ct_lo, b - 1)
                for o in range(KD):
                    last = nc.tensor.transpose(ps[:, 2 + b % 2, o * SEQ:o * SEQ + SEQ],
                                               c_tok[:, b % 2, o * P:o * P + P], ident)
                last.then_inc(ct_ready, 1)

            def scores(s):
                pe.wait_ge(ct_hi, 4 * s + 4)
                pe.wait_ge(ct_lo, 4 * s + 4)
                pe.wait_ge(wr_hi, 1)
                pe.wait_ge(wr_lo, 1)
                for k in range(KD):
                    for h in range(2):
                        last = nc.tensor.matmul(ps[:, 4], wr_st[:, k].rearrange("p h e -> p (h e)"),
                                                c_hl[:, h, k, halves(s)], start=(k == 0 and h == 0),
                                                stop=(k == KD - 1 and h == 1))
                last.then_inc(s_ready, 1)

            def turn_scores(s):
                pe.wait_ge(s_copied, s + 1)
                for t in range(4):
                    last = nc.tensor.matmul(ps[:, 5, t * EXPERTS:(t + 1) * EXPERTS], s_sb[:, t * P:t * P + P],
                                            ident2, start=True, stop=True)
                last.then_inc(score_ready, 1)

            def turn_gates(s):
                pe.wait_ge(gate_done, s + 1)
                if s:
                    pe.wait_ge(late_banks_free, 2)
                for t in range(4):
                    last = nc.tensor.transpose(ps[:, 6, t * P:t * P + P],
                                               gate2[:, t].rearrange("p c e -> p (c e)"), ident)
                last.then_inc(gate_tr, 1)

            def experts(n):
                j, s = H_ORDER[n]
                pe.wait_ge(am_hi, j + 1)
                pe.wait_ge(am_lo, j + 1)
                if n >= 4:
                    pe.wait_ge(hg_mul, n - 3)
                for k in range(KD):
                    last = mm3(ps[:, 2 * (j % 2) + s], am_hl[:, j % 4, 0, k], am_hl[:, j % 4, 1, k],
                               c_hl[:, 0, k, halves(s)], c_hl[:, 1, k, halves(s)], k == 0, k == KD - 1)
                last.then_inc(h_ready, 1)

            cond(0)
            for b in range(1, BATCH):
                cond(b)
                turn(b - 1)
                if b == 5:
                    scores(0)
                if b == 6:
                    turn_scores(0)
            pe.wait_ge(c_done, BATCH - 1)
            experts(0)
            turn(BATCH - 1)
            pe.wait_ge(ct_lo, BATCH - 1)
            experts(1)
            turn_gates(0)
            scores(1)
            experts(2)
            turn_scores(1)
            experts(3)
            experts(4)
            experts(5)
            turn_gates(1)
            for n in range(6, 2 * JT):
                experts(n)

            with pe.Fori(0, KD // 2) as i:
                for u in range(2):
                    o = 2 * i + u
                    pe.wait_ge(bm_hi, o + 1)
                    pe.wait_ge(bm_lo, o + 1)
                    for s in range(2):
                        pe.wait_ge(late_banks_free, 2 * o + s + 1)
                        for j in range(JT):
                            pe.wait_ge(hg_lo, 2 * JT - 2 + 2 * s if j >= JT - 2 else 2 * JT - 4)
                            last = mm3(ps[:, 4 + 2 * u + s], bm_hl[:, u, 0, j], bm_hl[:, u, 1, j],
                                       hg[:, j, 0, halves(s)], hg[:, j, 1, halves(s)], j == 0, j == JT - 1)
                        last.then_inc(o_ready, 1)


def constants():
    row, col = np.arange(P)[:, None], np.arange(PAIR)[None, :]
    own = (row % 32) // RANK == col // SEQ
    eye = np.eye(P)
    return np.concatenate([LORA_SCALE * own, eye, eye[:, :EXPERTS] + eye[:, EXPERTS:]], 1).astype(np.float32)


def features_first(w, tiles):
    return w.T.reshape(tiles, P, -1).transpose(1, 0, 2)


def kernel(x, itok_B_2_6, condB_coeff, mask_Bx4096x4096_ik1, L0_cond_W_gate, L0_cond_W_up, L0_cond_W_down,
           L0_cond_A_gate, L0_cond_B_gate, L0_cond_A_up, L0_cond_B_up, L0_cond_A_down, L0_cond_B_down,
           L0_ffn_lora_A, L0_ffn_lora_B, L0_ffn_W, L0_ffn_bias, L0_ffn_lora_weights, L1_cond_W, L1_cond_b,
           L1_ffn_A, L1_ffn_B, L1_ffn_Wr):
    import concourse.bacc as bacc
    from concourse.bass_utils import run_bass_kernel_spmd

    def pad_f(w, axis):
        widths = [(0, 0)] * w.ndim
        widths[axis] = (0, FPAD - F)
        return np.pad(w, widths)

    a = {k: np.asarray(v) for k, v in locals().items() if isinstance(v, np.ndarray) or hasattr(v, "dtype")}
    w_gu = np.stack([pad_f(a["L0_cond_W_gate"], 0), pad_f(a["L0_cond_W_up"], 0)])
    w_gu = w_gu.reshape(2, FT, P, KD, P).transpose(1, 4, 0, 3, 2)
    w_dn = pad_f(a["L0_cond_W_down"], 1).reshape(KD, P, FT, P).transpose(0, 3, 2, 1)
    b_t = {m: a[f"L0_cond_B_{m}"][0].transpose(0, 2, 1) for m in ("gate", "up", "down")}
    ins = {
        "x_t": features_first(a["x"].reshape(T, D), KD),
        "itok": a["itok_B_2_6"].reshape(1, BATCH),
        "coeff": a["condB_coeff"].reshape(1, BATCH),
        "mask_w": a["mask_Bx4096x4096_ik1"].reshape(BATCH, KD, P, D).transpose(0, 2, 1, 3),
        "w_gu": w_gu,
        "w_dn": w_dn,
        "a_gu": np.stack([a["L0_cond_A_gate"][0], a["L0_cond_A_up"][0]], 2),
        "a_dn": pad_f(a["L0_cond_A_down"][0], 2),
        "b_gu": np.stack([pad_f(b_t["gate"], 2), pad_f(b_t["up"], 2)], 1),
        "b_dn": b_t["down"],
        "lora_a": a["L0_ffn_lora_A"].reshape(P, D),
        "lora_b": a["L0_ffn_lora_B"].transpose(0, 2, 1).reshape(P, D),
        "lora_w": np.repeat(a["L0_ffn_lora_weights"], RANK).reshape(P, 1),
        "w0_t": features_first(a["L0_ffn_W"], KD),
        "bias0": a["L0_ffn_bias"].reshape(KD, P).T,
        "w1_t": features_first(a["L1_cond_W"], KD),
        "bias1": a["L1_cond_b"].reshape(1, D),
        "wr_t": features_first(a["L1_ffn_Wr"], KD),
        "a_moe": a["L1_ffn_A"].transpose(1, 0, 2).reshape(JT, P, KD, P).transpose(0, 3, 2, 1),
        "b_moe": a["L1_ffn_B"].transpose(2, 0, 1).reshape(JT, P, KD, P).transpose(2, 1, 0, 3),
        "consts": constants(),
    }
    ins = {k: np.ascontiguousarray(v) for k, v in ins.items()}
    nc = bacc.Bacc("TRN2", target_bir_lowering=False, num_devices=1)
    args = [nc.dram_tensor(k, v.shape, mybir.dt.from_np(v.dtype), kind="ExternalInput").ap() for k, v in ins.items()]
    out = nc.dram_tensor("out", (KD, P, T), F32, kind="ExternalOutput").ap()
    build(nc, *args, out)
    r = run_bass_kernel_spmd(nc, [ins], core_ids=[0])
    return r.results[0]["out"].reshape(D, T).T.reshape(BATCH, SEQ, D)
```

```python
from contextlib import ExitStack

import numpy as np

import concourse.bass as bass
from concourse import mybir

F32 = mybir.dt.float32
F32R = mybir.dt.float32r
I32 = mybir.dt.int32
ALU = mybir.AluOpType
ACT = mybir.ActivationFunctionType
AX_X = mybir.AxisListType.X

P = 128
BATCH, SEQ, D = 8, 128, 512
T = BATCH * SEQ
KD = D // P
HALF = T // 2
PAIR = 2 * SEQ
NPAIR = BATCH // 2
F = 1376
FT = -(-F // P)
FPAD = FT * P
RANK = 16
ADAPTERS = 16
LORA_SCALE = 0.5
FFN_SCALE = 2.0
MOE_SCALE = 2.0
EXPERTS = 64
TOPK = 16
JT = EXPERTS * RANK // P
PREP = 5
DVE_SPLITS = 4
WC_RAW = 4
W0_AFTER = ((0, 1), (2,), (3,), ())
NEG = -3.0e38
A_BY_POOL = 7
WARM_UP = 9
KB = 1024
AM_SLOTS = 4
H_ORDER = [(j + dj, s) for j in range(0, JT, AM_SLOTS) for s in range(2) for dj in range(AM_SLOTS)]
HALF_TAIL = len(H_ORDER) - AM_SLOTS


def build(nc, x_t, itok, coeff, mask_w, w_gu, w_dn, a_gu, a_dn, b_gu, b_dn,
          lora_a, lora_b, lora_w, w0_t, bias0, w1_t, bias1, wr_t, a_moe, b_moe, consts, out):
    with ExitStack() as ctx:
        base = -(-nc.sbuf_base // 32) * 32

        def sem(name):
            return ctx.enter_context(nc.semaphore(name))

        def at(name, shape, dtype, offset):
            return nc.alloc_sbuf_tensor_at(name, shape, dtype, offset=base + offset)

        R_CONST = 0
        R_X = R_CONST + 11 * KB // 4
        R_U = R_X + 32 * KB
        R_T = R_U + 40 * KB
        R_S = R_T + 8 * KB
        R_AD = R_S + 4 * KB
        R_ACT = R_AD + 32 * KB
        assert base + R_ACT + 88 * KB <= nc.sbuf_usable_end

        const_sb = at("const_sb", [P, 448], F32, R_CONST)
        block_mask = const_sb[:, 0:PAIR]
        ident = const_sb[:, PAIR:PAIR + P]
        ident2 = const_sb[:, PAIR + P:PAIR + P + EXPERTS]
        small = R_CONST + 448 * 4
        bias0_sb = at("bias0_sb", [P, KD], F32, small)
        lora_w_sb = at("lora_w_sb", [P, 1], F32, small + 32)
        coeff_sb = at("coeff_sb", [P, BATCH], F32, small + 64)
        coeff2 = at("coeff2", [P, BATCH], F32, small + 96)
        coeff_neg = at("coeff_neg", [P, BATCH], F32, small + 128)
        itok_sb = at("itok_sb", [1, BATCH], I32, small + 160)
        top8 = at("top8", [P, 4, 2, 8], F32, small + 192)
        gate_sum = at("gate_sum", [P, 4], F32, small + 448)
        gate_inv = at("gate_inv", [P, 4], F32, small + 480)

        def slots(name, shape, dtype, offset):
            return [at(f"{name}{u}", shape, dtype, R_U + 20 * KB * u + offset) for u in range(2)]

        x_hl = at("x_hl", [P, 2, KD, T], F32R, R_X)
        w_hl = slots("w_hl", [P, 2, 2, KD, P], F32R, 0)
        w_raw = slots("w_raw", [P, 2, KD, P], F32, 8 * KB)
        b_raw = slots("b_raw", [P, 2, NPAIR, P], F32, 12 * KB)
        b_st = slots("b_st", [P, 2, NPAIR, P], F32R, 16 * KB)
        t_st = at("t_st", [P, NPAIR, 2, PAIR], F32R, R_T)
        glu = at("glu", [P, 2, HALF], F32, R_S)
        act = at("act", [P, FT * 2 * T], F32R, R_ACT)
        st = R_ACT + 40 * KB
        x_raw = at("x_raw", [P, KD, T], F32, st)
        a_nat = at("a_nat", [P, 2, D], F32, st + 16 * KB)
        a_st = at("a_st", [P, KD * NPAIR, 2, 2, 32], F32R, st + 20 * KB)
        t_raw = at("t_raw", [P, NPAIR, PAIR], F32, st + 28 * KB)
        warm = at("warm", [P, P + 1], F32, st + 32 * KB)
        ad_st = at("ad_st", [P, FT * NPAIR, 4, 32], F32R, R_AD)
        ad_nat = at("ad_nat", [P, FPAD], F32, R_AD + 22 * KB)
        wd_raw = at("wd_raw", [P, 2, D], F32, R_T + 4 * KB)
        wd_hl = at("wd_hl", [P, 2, 2, D], F32R, R_X + 16 * KB)
        bd_raw = at("bd_raw", [P, NPAIR, D], F32, R_U)
        bd_st = at("bd_st", [P, NPAIR, D], F32R, R_X + 24 * KB)
        td_st = at("td_st", [P, NPAIR, PAIR], F32R, R_T)
        td_raw = at("td_raw", [P, NPAIR, PAIR], F32, R_S)
        d_hl = at("d_hl", [P, 2, KD, T], F32R, R_U)
        la_hl = at("la_hl", [P, 2, D], F32R, R_U + 20 * KB)
        lb_hl = at("lb_hl", [P, 2, D], F32R, R_U + 24 * KB)
        la_raw = at("la_raw", [P, D], F32, R_U + 28 * KB)
        lb_raw = at("lb_raw", [P, D], F32, R_U + 30 * KB)
        w0_raw = at("w0_raw", [P, KD, D], F32, R_U + 32 * KB)
        w0_hl = at("w0_hl", [P, 2, KD, D], F32R, R_X)
        x2 = at("x2", [P, KD, T], F32, R_ACT + 56 * KB)
        w1_raw = at("w1_raw", [P, KD, D], F32, R_AD + 16 * KB)
        wc_raw = [at(f"wc_raw{n}", [P, KD, D], F32, place) for n, place in enumerate(
            (R_AD, R_AD + 8 * KB, R_AD + 24 * KB, R_U + 32 * KB))]
        wc_hl = [at(f"wc_hl{n}", [P, 2, KD, D], F32R, place) for n, place in enumerate(
            (R_ACT, R_ACT + 16 * KB, R_ACT + 32 * KB, R_X + 16 * KB, R_X))]
        bias1_sb = at("bias1_sb", [P, D], F32, R_ACT + 48 * KB)
        xs_hl = at("xs_hl", [P, 2, 2, KD, SEQ], F32R, R_T)
        c_tok = at("c_tok", [P, 2, D], F32, R_S)
        c_hl = at("c_hl", [P, 2, KD, T], F32R, R_U)
        wr_raw = at("wr_raw", [P, KD, EXPERTS], F32, R_ACT + 54 * KB)
        wr_st = at("wr_st", [P, KD, 2, EXPERTS], F32R, R_ACT + 50 * KB)
        s_sb = at("s_sb", [P, HALF], F32, R_ACT + 52 * KB)
        score = at("score", [P, 4, EXPERTS], F32, R_AD + 12 * KB)
        left1 = at("left1", [P, 4, EXPERTS], F32, R_AD + 13 * KB)
        left2 = at("left2", [P, 4, EXPERTS], F32, R_AD + 14 * KB)
        expo = at("expo", [P, 4, EXPERTS], F32, R_AD + 15 * KB)
        gate2 = at("gate2", [P, 4, 2, EXPERTS], F32, R_ACT + 54 * KB)
        gate_x = at("gate_x", [P, 2, HALF], F32, R_AD)
        am_raw = at("am_raw", [P, 2, KD, P], F32, R_AD + 4 * KB)
        am_hl = at("am_hl", [P, AM_SLOTS, 2, KD, P], F32R, R_X)
        hg_raw = at("hg_raw", [P, 2, HALF], F32, R_AD + 8 * KB)
        hg = [at(f"hg{n}", [P, 2, 2, T], F32R, place) for n, place in enumerate(
            (R_X + 16 * KB, R_ACT, R_ACT + 16 * KB, R_ACT + 32 * KB))]
        bm_raw = at("bm_raw", [P, 2, JT, P], F32, R_U + 32 * KB)
        bm_hl = at("bm_hl", [P, 2, 2, JT, P], F32R, R_AD + 16 * KB)

        ps = ctx.enter_context(nc.psum_tensor("ps", [P, 8, 512], F32))

        b_sel = nc.dram_tensor("b_sel", (2, P, FPAD), F32).ap()
        bd_sel = nc.dram_tensor("bd_sel", (P, D), F32).ap()

        dma_itok, dma_const, dma_small = sem("dma_itok"), sem("dma_const"), sem("dma_small")
        dma_w_first = [sem(f"dma_w_first{k}") for k in range(KD)]
        warm_set = sem("warm_set")
        dma_x0 = [sem(f"dma_x0_{k}") for k in range(KD)]
        dma_x1 = [sem(f"dma_x1_{k}") for k in range(KD)]
        dma_w = [sem(f"dma_w{u}") for u in range(2)]
        dma_b = [sem(f"dma_b{u}") for u in range(2)]
        dma_a, dma_a_sp, dma_bsel, dma_ad, dma_bdsel = sem("dma_a"), sem("dma_a_sp"), sem("dma_bsel"), sem("dma_ad"), sem("dma_bdsel")
        dma_wd = [sem(f"dma_wd{u}") for u in range(2)]
        dma_bd, dma_lora, dma_ffn_w = sem("dma_bd"), sem("dma_lora"), sem("dma_ffn_w")
        dma_x2 = [sem(f"dma_x2_{s}") for s in range(2)]
        dma_mask = [sem(f"dma_mask{u}") for u in range(WC_RAW)]
        dma_cond_w, dma_l1 = sem("dma_cond_w"), sem("dma_l1")
        dma_am = [sem(f"dma_am{u}") for u in range(2)]
        dma_bm = [sem(f"dma_bm{u}") for u in range(2)]
        dma_out = sem("dma_out")
        x_hi, x_lo = sem("x_hi"), sem("x_lo")
        w_hi, w_lo, b_hi, b_lo = sem("w_hi"), sem("w_lo"), sem("b_hi"), sem("b_lo")
        a_tr, a_hi, a_lo = sem("a_tr"), sem("a_hi"), sem("a_lo")
        t_ready, t_masked, t_hi, t_lo = sem("t_ready"), sem("t_masked"), sem("t_hi"), sem("t_lo")
        gate_ready, up_ready = sem("gate_ready"), sem("up_ready")
        silu_done, glu_done, act_hi, act_lo = sem("silu_done"), sem("glu_done"), sem("act_hi"), sem("act_lo")
        ad_tr, ad_hi, ad_lo = sem("ad_tr"), sem("ad_hi"), sem("ad_lo")
        td_ready, td_masked, td_hi, td_lo = sem("td_ready"), sem("td_masked"), sem("td_hi"), sem("td_lo")
        wd_hi, wd_lo, bd_hi, bd_lo = sem("wd_hi"), sem("wd_lo"), sem("bd_hi"), sem("bd_lo")
        down_tiles, d_ready, d_hi, d_lo = sem("down_tiles"), sem("d_ready"), sem("d_hi"), sem("d_lo")
        lb_scaled, lora_hi, lora_lo = sem("lb_scaled"), sem("lora_hi"), sem("lora_lo")
        w0_ready, w0_sum, w0_hi, w0_lo = sem("w0_ready"), sem("w0_sum"), sem("w0_hi"), sem("w0_lo")
        x2_ready, x2_done = sem("x2_ready"), sem("x2_done")
        coeff_done, wc_formed, wc_added = sem("coeff_done"), sem("wc_formed"), sem("wc_added")
        wc_hi, xs_hi, xs_lo = sem("wc_hi"), sem("xs_hi"), sem("xs_lo")
        wc_lo, wc_lo_late = sem("wc_lo"), sem("wc_lo_late")
        c_ready, c_done, ct_ready, ct_hi, ct_lo = sem("c_ready"), sem("c_done"), sem("ct_ready"), sem("ct_hi"), sem("ct_lo")
        wr_hi, wr_lo = sem("wr_hi"), sem("wr_lo")
        s_ready, s_copied, score_ready = sem("s_ready"), sem("s_copied"), sem("score_ready")
        top_step, shifted, exp_done, gate_done = sem("top_step"), sem("shifted"), sem("exp_done"), sem("gate_done")
        gate_tr, late_banks_free = sem("gate_tr"), sem("late_banks_free")
        am_hi, am_lo, h_ready, hg_mul, hg_hi, hg_lo = (sem("am_hi"), sem("am_lo"), sem("h_ready"), sem("hg_mul"),
                                                      sem("hg_hi"), sem("hg_lo"))
        bm_hi, bm_lo, o_ready = sem("bm_hi"), sem("bm_lo"), sem("o_ready")

        def rows3(v):
            return v.unsqueeze(2).broadcast_to([P, v.shape[1], 3, 32])

        block = ctx.enter_context(nc.Block())

        @block.sync
        def _(sp):
            for k in range(KD):
                sp.dma_start(x_raw[:, k, 0:HALF], x_t[:, k, 0:HALF]).then_inc(dma_x0[k], 16)
                if k == 0:
                    sp.dma_start(itok_sb[:], itok).then_inc(dma_itok, 16)
                else:
                    sp.dma_start(w_raw[0][:, :, k], w_gu[0, :, :, k]).then_inc(dma_w_first[k], 16)
            sp.wait_ge(dma_itok, 16)
            for b in range(A_BY_POOL, BATCH):
                adapter = sp.value_load(itok_sb[0:1, b:b + 1], min_val=0, max_val=ADAPTERS - 1)
                sp.dma_start(a_nat[RANK * b:RANK * b + RANK], a_gu[bass.ds(adapter, 1)]).then_inc(dma_a_sp, 16)
            for k in range(KD):
                sp.dma_start(x_raw[:, k, HALF:T], x_t[:, k, HALF:T]).then_inc(dma_x1[k], 16)
            sp.dma_start(const_sb[:], consts).then_inc(dma_const, 16)
            sp.dma_start(w_raw[1][:], w_gu[1]).then_inc(dma_w[1], 16)
            for b in range(BATCH):
                adapter = sp.value_load(itok_sb[0:1, b:b + 1], min_val=0, max_val=ADAPTERS - 1)
                sp.dma_start(b_sel[:, RANK * b:RANK * b + RANK], b_gu[bass.ds(adapter, 1)]).then_inc(dma_bsel, 16)

            def load_b(cols, slot):
                for q in range(4):
                    src = b_sel.rearrange("m (p r) f -> r (m p) f", p=NPAIR)[:, :, cols]
                    dst = b_raw[slot][32 * q:32 * q + 32].rearrange("r m p f -> r (m p) f")
                    sp.dma_start(dst, src).then_inc(dma_b[slot], 16)

            sp.wait_ge(dma_bsel, 16 * BATCH)
            load_b(slice(0, P), 0)
            load_b(slice(P, 2 * P), 1)
            sp.dma_start(bias0_sb[:], bias0).then_inc(dma_small, 16)
            sp.dma_start(lora_w_sb[:], lora_w).then_inc(dma_small, 16)
            sp.dma_start(coeff_sb[:], coeff.partition_broadcast(P)).then_inc(dma_small, 16)

            def load_tile(f, slot):
                for made in (w_hi, w_lo):
                    sp.wait_ge(made, KD + f - 2)
                sp.dma_start(w_raw[slot][:], w_gu[bass.ds(f, 1)]).then_inc(dma_w[slot], 16)
                sp.wait_ge(b_hi, f - 1)
                sp.wait_ge(b_lo, 2 * f - 2)
                load_b(bass.ds(f * P, P), slot)

            with sp.Fori(0, (FT - 3) // 2) as i:
                for u in range(2):
                    load_tile(2 * i + 2 + u, u)
            load_tile(FT - 1, 0)

            sp.wait_ge(up_ready, 2 * FT - 2)
            sp.dma_start(la_raw[:], lora_a).then_inc(dma_lora, 16)
            sp.dma_start(lb_raw[:], lora_b).then_inc(dma_lora, 16)
            sp.dma_start(w0_raw[:], w0_t).then_inc(dma_ffn_w, 16)
            sp.wait_ge(up_ready, 2 * FT)
            for f in range(2):
                sp.dma_start(wd_raw[:, f], w_dn[f]).then_inc(dma_wd[f], 16)
            sp.wait_ge(dma_bdsel, 16 * BATCH)
            for q in range(4):
                sp.dma_start(bd_raw[32 * q:32 * q + 32], bd_sel.rearrange("(p r) o -> r p o", p=NPAIR)).then_inc(dma_bd, 16)

            def load_wd(f):
                sp.wait_ge(wd_hi, f - 1)
                sp.wait_ge(wd_lo, f - 1)
                sp.dma_start(wd_raw[:, f % 2], w_dn[f]).then_inc(dma_wd[f % 2], 16)

            def load_mask(b):
                if b >= WC_RAW:
                    sp.wait_ge(wc_lo, b - WC_RAW + 1)
                    sp.wait_ge(wc_hi, b - WC_RAW + 1)
                elif b == 3:
                    sp.wait_ge(w0_lo, KD)
                    sp.wait_ge(w0_hi, KD)
                sp.dma_start(wc_raw[b % WC_RAW][:].bitcast(I32), mask_w[b]).then_inc(dma_mask[b % WC_RAW], 16)

            load_wd(2)
            load_wd(3)
            sp.wait_ge(ad_tr, FT)
            sp.wait_ge(td_ready, NPAIR)
            load_mask(0)
            sp.dma_start(w1_raw[:], w1_t).then_inc(dma_cond_w, 16)
            load_mask(1)
            load_wd(4)
            load_mask(2)
            load_wd(5)
            load_mask(3)
            for f in range(6, FT):
                load_wd(f)
                if f == 9:
                    load_mask(4)
            sp.wait_ge(down_tiles, 7)
            sp.dma_start(bias1_sb[:], bias1.partition_broadcast(P)).then_inc(dma_l1, 16)
            sp.dma_start(wr_raw[:], wr_t).then_inc(dma_l1, 16)
            load_mask(5)
            sp.wait_ge(d_ready, 2 * KD)
            for s in range(2):
                half = slice(s * HALF, s * HALF + HALF)
                sp.dma_start(x2[:, :, half], x_t[:, :, half]).then_inc(dma_x2[s], 16)
            load_mask(6)
            load_mask(7)

            def load_am(j):
                if j >= 2:
                    sp.wait_ge(am_hi, j - 1)
                    sp.wait_ge(am_lo, j - 1)
                sp.dma_start(am_raw[:, j % 2], a_moe[j]).then_inc(dma_am[j % 2], 16)

            sp.wait_ge(wc_hi, 5)
            sp.wait_ge(wc_lo_late, 5 - DVE_SPLITS)
            for j in range(4):
                load_am(j)
            sp.wait_ge(wc_hi, BATCH)
            sp.wait_ge(wc_lo_late, BATCH - DVE_SPLITS)
            for o in range(2):
                sp.dma_start(bm_raw[:, o], b_moe[o]).then_inc(dma_bm[o], 16)
            for j in range(4, JT):
                load_am(j)
            for o in range(2, KD):
                sp.wait_ge(bm_hi, o - 1)
                sp.wait_ge(bm_lo, o - 1)
                sp.dma_start(bm_raw[:, o % 2], b_moe[o]).then_inc(dma_bm[o % 2], 16)
            for n in range(2 * KD):
                o, s = n // 2, n % 2
                sp.wait_ge(late_banks_free, 4 + n + 1)
                half = slice(s * HALF, s * HALF + HALF)
                sp.dma_start(out[o, :, half], x2[:, o, half]).then_inc(dma_out, 16)
            sp.wait_ge(dma_out, 16 * 2 * KD)

        @block.gpsimd
        def _(pool):
            pool.dma_start(w_raw[0][:, :, 0], w_gu[0, :, :, 0]).then_inc(dma_w_first[0], 16)
            pool.wait_ge(dma_itok, 16)
            adapters = []
            for b in range(BATCH):
                adapters.append(pool.value_load(itok_sb[0:1, b:b + 1], min_val=0, max_val=ADAPTERS - 1))
                if b >= A_BY_POOL:
                    continue
                pool.dma_start(a_nat[RANK * b:RANK * b + RANK], a_gu[bass.ds(adapters[b], 1)]).then_inc(dma_a, 16)
            for b in range(BATCH):
                pool.dma_start(ad_nat[RANK * b:RANK * b + RANK], a_dn[bass.ds(adapters[b], 1)]).then_inc(dma_ad, 16)
            for b in range(BATCH):
                pool.dma_start(bd_sel[RANK * b:RANK * b + RANK], b_dn[bass.ds(adapters[b], 1)]).then_inc(dma_bdsel, 16)
            pool.wait_ge(dma_cond_w, 16)
            for b in range(BATCH):
                pool.wait_ge(wc_formed, b + 1)
                wc = wc_raw[b % WC_RAW]
                nc.gpsimd.tensor_tensor(wc[:], wc[:], w1_raw[:], ALU.add).then_inc(wc_added, 1)

            for b in range(DVE_SPLITS, BATCH):
                pool.wait_ge(wc_hi, b + 1)
                wc, wc_split = wc_raw[b % WC_RAW], wc_hl[b % PREP]
                nc.gpsimd.tensor_tensor(wc_split[:, 1], wc[:], wc_split[:, 0].bitcast(F32),
                                        ALU.subtract).then_inc(wc_lo_late, 1)

            def am_low(j):
                pool.wait_ge(am_hi, j + 1)
                nc.gpsimd.tensor_tensor(am_hl[:, j % AM_SLOTS, 1], am_raw[:, j % 2], am_hl[:, j % AM_SLOTS, 0].bitcast(F32),
                                        ALU.subtract).then_inc(am_lo, 1)

            def bm_low(o):
                pool.wait_ge(bm_hi, o + 1)
                nc.gpsimd.tensor_tensor(bm_hl[:, o % 2, 1], bm_raw[:, o % 2], bm_hl[:, o % 2, 0].bitcast(F32),
                                        ALU.subtract).then_inc(bm_lo, 1)

            for j in range(JT):
                am_low(j)
            for o in range(KD):
                bm_low(o)

        @block.scalar
        def _(act_e):
            def copy(out, in_):
                return nc.scalar.activation(out, in_, ACT.Copy)

            def x_high(k, s):
                if s == 0:
                    act_e.wait_ge(dma_x0[k], 16)
                else:
                    act_e.wait_ge(dma_x1[k], 16)
                half = slice(s * HALF, s * HALF + HALF)
                copy(x_hl[:, 0, k, half], x_raw[:, k, half]).then_inc(x_hi, 1)

            def split_w(f, slot, use):
                act_e.wait_ge(dma_w[slot], 16 * (use - 1 if slot == 0 else use))
                if not isinstance(f, int) or f >= 2:
                    act_e.wait_ge(up_ready, 2 * f - 2)
                copy(w_hl[slot][:, 0], w_raw[slot][:]).then_inc(w_hi, 1)

            def split_b(f, slot, use):
                act_e.wait_ge(dma_b[slot], 64 * use)
                copy(b_st[slot][:], b_raw[slot][:]).then_inc(b_hi, 1)

            def split(f, slot, use):
                split_w(f, slot, use)
                split_b(f, slot, use)

            def evacuate(f, bank, first=False):
                for s in range(2):
                    act_e.wait_ge(gate_ready, 2 * f + s + 1)
                    if not first:
                        act_e.wait_ge(act_lo, 2 * f + s - 1)
                    nc.scalar.activation(glu[:, s], ps[:, 4 * bank + 2 * s], ACT.Silu).then_inc(silu_done, 1)
                    act_e.wait_ge(glu_done, 2 * f + s + 1)
                    copy(act[:, bass.ds(f * (2 * T) + s * HALF, HALF)], glu[:, s]).then_inc(act_hi, 1)

            act_e.wait_ge(warm_set, 1)
            nc.scalar.activation(warm[:, P:P + 1], warm[:, 0:1], ACT.Silu)
            for k in range(KD):
                x_high(k, 0)
                act_e.wait_ge(dma_w_first[k], 16)
                copy(w_hl[0][:, 0, :, k], w_raw[0][:, :, k]).then_inc(w_hi, 1)
            for k in range(KD):
                x_high(k, 1)
            split_w(1, 1, 1)
            for m in range(2):
                act_e.wait_ge(a_tr, KD * (m + 1))
                copy(a_st[:, :, m, 0, :], ps[:, 4 + m].rearrange("p (n c) -> p n c", c=32)).then_inc(a_hi, 1)
            for p in range(NPAIR):
                act_e.wait_ge(t_masked, p + 1)
                copy(t_st[0:64, p, 0], t_raw[0:64, p]).then_inc(t_hi, 1)
                copy(t_st[64:128, p, 1], t_raw[64:128, p]).then_inc(t_hi, 1)
                copy(t_st[64:96, p, 0], t_raw[0:32, p]).then_inc(t_hi, 1)
                copy(t_st[0:32, p, 1], t_raw[64:96, p]).then_inc(t_hi, 1)
            split_b(0, 0, 1)
            split_b(1, 1, 1)
            split(2, 0, 2)
            evacuate(0, 0, first=True)
            evacuate(1, 1)
            with act_e.Fori(0, (FT - 3) // 2) as i:
                for u in range(2):
                    split(2 * i + 3 + u, 1 - u, i + 2 + u)
                    evacuate(2 * i + 2 + u, u)
            act_e.wait_ge(up_ready, 2 * FT - 2)
            act_e.wait_ge(dma_lora, 32)
            copy(la_hl[:, 0], la_raw[:]).then_inc(lora_hi, 1)
            act_e.wait_ge(lb_scaled, 1)
            copy(lb_hl[:, 0], lb_raw[:]).then_inc(lora_hi, 1)
            for g in range(3):
                n = min(4, FT - 4 * g)
                act_e.wait_ge(ad_tr, 4 * g + n)
                copy(ad_st[:, 16 * g:16 * g + 4 * n, 0:3, :],
                     rows3(ps[:, 4 + g, 0:n * P].rearrange("p (n c) -> p n c", c=32))).then_inc(ad_hi, 1)
            evacuate(FT - 1, 0)

            def wd_high(f):
                act_e.wait_ge(dma_wd[f % 2], 16 * (f // 2 + 1))
                if f < 2:
                    act_e.wait_ge(up_ready, 2 * FT)
                else:
                    act_e.wait_ge(down_tiles, f - 1)
                copy(wd_hl[:, f % 2, 0], wd_raw[:, f % 2]).then_inc(wd_hi, 1)

            def form(b):
                act_e.wait_ge(dma_mask[b % WC_RAW], 16 * (b // WC_RAW + 1))
                act_e.wait_ge(coeff_done, 2)
                wc = wc_raw[b % WC_RAW]
                nc.scalar.activation(wc[:], wc[:].bitcast(I32), ACT.Identity, bias=coeff_neg[:, b:b + 1],
                                     scale=coeff2[:, b:b + 1]).then_inc(wc_formed, 1)

            def wc_high(b):
                act_e.wait_ge(wc_added, b + 1)
                if b < 3:
                    act_e.wait_ge(down_tiles, 2 * b + 2)
                elif b == 3:
                    act_e.wait_ge(d_ready, 2 * KD)
                elif b == 4:
                    act_e.wait_ge(x2_ready, 2 * KD)
                else:
                    act_e.wait_ge(c_ready, b - PREP + 1)
                copy(wc_hl[b % PREP][:, 0], wc_raw[b % WC_RAW][:]).then_inc(wc_hi, 1)

            def xs_high(b):
                act_e.wait_ge(x2_done, KD if b < BATCH // 2 else 2 * KD)
                if b >= 2:
                    act_e.wait_ge(c_ready, b - 1)
                copy(xs_hl[:, b % 2, 0], x2[:, :, b * SEQ:b * SEQ + SEQ]).then_inc(xs_hi, 1)

            def ct_high(b):
                act_e.wait_ge(ct_ready, b + 1)
                copy(c_hl[:, 0, :, b * SEQ:b * SEQ + SEQ],
                     ps[:, 2 + b % 2].rearrange("p (o t) -> p o t", t=SEQ)).then_inc(ct_hi, 1)

            def am_high(j):
                act_e.wait_ge(dma_am[j % 2], 16 * (j // 2 + 1))
                if j < AM_SLOTS:
                    act_e.wait_ge(c_ready, 5)
                else:
                    act_e.wait_ge(h_ready, H_ORDER.index((j - AM_SLOTS, 1)) + 1)
                copy(am_hl[:, j % AM_SLOTS, 0], am_raw[:, j % 2]).then_inc(am_hi, 1)

            def s_copy(s):
                act_e.wait_ge(s_ready, s + 1)
                copy(s_sb[:], ps[:, 4]).then_inc(s_copied, 1)

            def exponent(s):
                act_e.wait_ge(shifted, s + 1)
                nc.scalar.activation(expo[:], expo[:], ACT.Exp).then_inc(exp_done, 1)

            def gate_copy(s):
                act_e.wait_ge(gate_tr, s + 1)
                copy(gate_x[:, s], ps[:, 6]).then_inc(late_banks_free, 2)

            wd_high(0)
            wd_high(1)
            for k in range(KD):
                act_e.wait_ge(w0_sum, k + 1)
                copy(w0_hl[:, 0, k], w0_raw[:, k]).then_inc(w0_hi, 1)
            for p in range(NPAIR):
                act_e.wait_ge(td_masked, p + 1)
                copy(td_st[:, p], td_raw[:, p]).then_inc(td_hi, 1)
            act_e.wait_ge(dma_bd, 64)
            copy(bd_st[:], bd_raw[:]).then_inc(bd_hi, 1)
            after = {0: [(form, 0)], 1: [(form, 1)], 2: [(wc_high, 0)], 3: [(form, 2)], 4: [(wc_high, 1), (form, 3)],
                     6: [(wc_high, 2)], 7: [(form, 4)], 8: [(form, 5)]}
            for f in range(2, FT):
                wd_high(f)
                for do, b in after.get(f - 2, []):
                    do(b)
            for s in range(2):
                for o in range(KD):
                    act_e.wait_ge(d_ready, KD * s + o + 1)
                    copy(d_hl[:, 0, o, s * HALF:s * HALF + HALF], ps[:, 4 * s + o]).then_inc(d_hi, 1)
            act_e.wait_ge(dma_l1, 32)
            copy(wr_st[:, :, 0], wr_raw[:]).then_inc(wr_hi, 1)
            wc_high(3)
            form(6)
            form(7)
            xs_high(0)
            xs_high(1)
            wc_high(4)
            for b in range(BATCH):
                if b + 2 < BATCH:
                    xs_high(b + 2)
                if b:
                    ct_high(b - 1)
                if b + PREP < BATCH:
                    wc_high(b + PREP)
                if b == 6:
                    am_high(0)
                    am_high(1)
                if b == 5:
                    s_copy(0)
            ct_high(BATCH - 1)
            exponent(0)
            am_high(2)
            am_high(3)

            def hg_high(n):
                j, s = H_ORDER[n]
                act_e.wait_ge(hg_mul, n + 1)
                copy(hg[j // 2][:, j % 2, 0, s * HALF:s * HALF + HALF], hg_raw[:, n % 2]).then_inc(hg_hi, 1)

            def bm_high(o):
                act_e.wait_ge(dma_bm[o % 2], 16 * (o // 2 + 1))
                if o >= 2:
                    act_e.wait_ge(o_ready, 2 * o - 2)
                copy(bm_hl[:, o % 2, 0], bm_raw[:, o % 2]).then_inc(bm_hi, 1)

            s_copy(1)
            gate_copy(0)
            exponent(1)
            for n in range(4):
                hg_high(n)
            gate_copy(1)
            for n in range(4, 2 * JT):
                if 4 <= n < 8:
                    am_high(n)
                hg_high(n)
                if n in (8, 10):
                    bm_high((n - 8) // 2)
            for o in range(2, KD):
                bm_high(o)

        @block.vector
        def _(dve):
            def low(out, whole, high):
                return nc.vector.tensor_tensor(out, whole, high.bitcast(F32), ALU.subtract)

            def x_low(k, s):
                n = KD * s + k
                dve.wait_ge(x_hi, n + 1)
                half = slice(s * HALF, s * HALF + HALF)
                low(x_hl[:, 1, k, half], x_raw[:, k, half], x_hl[:, 0, k, half]).then_inc(x_lo, 1)

            def w_low(f, slot):
                dve.wait_ge(w_hi, KD + f)
                low(w_hl[slot][:, 1], w_raw[slot][:], w_hl[slot][:, 0]).then_inc(w_lo, 1)

            def b_low(f, slot):
                dve.wait_ge(b_hi, f + 1)
                for m, rows in enumerate((slice(64, 96), slice(0, 32))):
                    low(b_st[slot][rows, m], b_raw[slot][rows, m], b_st[slot][rows, m]).then_inc(b_lo, 1)

            def evacuate(f, bank):
                for s in range(2):
                    dve.wait_ge(silu_done, 2 * f + s + 1)
                    dve.wait_ge(up_ready, 2 * f + s + 1)
                    done = nc.vector.tensor_tensor(glu[:, s], glu[:, s], ps[:, 4 * bank + 2 * s + 1], ALU.mult)
                    done.then_inc(glu_done, 1)
                    dve.wait_ge(act_hi, 2 * f + s + 1)
                    low(act[:, bass.ds(f * (2 * T) + T + s * HALF, HALF)], glu[:, s],
                        act[:, bass.ds(f * (2 * T) + s * HALF, HALF)]).then_inc(act_lo, 1)

            nc.vector.memset(warm[:], 0.0).then_inc(warm_set, 1)
            for k in range(KD):
                x_low(k, 0)
                dve.wait_ge(w_hi, k + 1)
                low(w_hl[0][:, 1, :, k], w_raw[0][:, :, k], w_hl[0][:, 0, :, k]).then_inc(w_lo, 1)
            for k in range(KD):
                x_low(k, 1)
            w_low(1, 1)
            for m in range(2):
                dve.wait_ge(a_hi, m + 1)
                low(a_st[:, :, m, 1, :], ps[:, 4 + m].rearrange("p (n c) -> p n c", c=32),
                    a_st[:, :, m, 0, :]).then_inc(a_lo, 1)
            dve.wait_ge(dma_const, 16)

            def t_mask(p):
                dve.wait_ge(t_ready, p + 1)
                nc.vector.tensor_tensor(t_raw[:, p], ps[:, 4 + p, 0:PAIR], block_mask, ALU.mult).then_inc(t_masked, 1)

            def t_low(p):
                dve.wait_ge(t_hi, 4 * p + 2)
                low(t_st[96:128, p, 0], t_raw[0:32, p], t_st[0:32, p, 0]).then_inc(t_lo, 1)
                low(t_st[32:64, p, 1], t_raw[64:96, p], t_st[64:96, p, 1]).then_inc(t_lo, 1)

            for p in range(NPAIR):
                t_mask(p)
                if p:
                    t_low(p - 1)
            t_low(NPAIR - 1)
            b_low(0, 0)
            b_low(1, 1)
            w_low(2, 0)
            b_low(2, 0)
            evacuate(0, 0)
            evacuate(1, 1)
            with dve.Fori(0, (FT - 3) // 2) as i:
                for u in range(2):
                    w_low(2 * i + 3 + u, 1 - u)
                    b_low(2 * i + 3 + u, 1 - u)
                    evacuate(2 * i + 2 + u, u)
            dve.wait_ge(dma_small, 48)
            dve.wait_ge(dma_lora, 32)
            nc.vector.tensor_scalar(lb_raw[:], lb_raw[:], lora_w_sb[:, 0:1], FFN_SCALE, ALU.mult,
                                    ALU.mult).then_inc(lb_scaled, 1)
            dve.wait_ge(lora_hi, 1)
            low(la_hl[:, 1], la_raw[:], la_hl[:, 0]).then_inc(lora_lo, 1)
            dve.wait_ge(lora_hi, 2)
            low(lb_hl[:, 1], lb_raw[:], lb_hl[:, 0]).then_inc(lora_lo, 1)
            nc.vector.tensor_scalar(coeff2[:], coeff_sb[:], 2.0, None, ALU.mult).then_inc(coeff_done, 1)
            nc.vector.tensor_scalar(coeff_neg[:], coeff_sb[:], -1.0, None, ALU.mult).then_inc(coeff_done, 1)
            for g in range(3):
                n = min(4, FT - 4 * g)
                dve.wait_ge(ad_hi, g + 1)
                low(ad_st[:, 16 * g:16 * g + 4 * n, 3, :], ps[:, 4 + g, 0:n * P].rearrange("p (n c) -> p n c", c=32),
                    ad_st[:, 16 * g:16 * g + 4 * n, 0, :]).then_inc(ad_lo, 1)
            evacuate(FT - 1, 0)

            def wd_low(f):
                dve.wait_ge(wd_hi, f + 1)
                low(wd_hl[:, f % 2, 1], wd_raw[:, f % 2], wd_hl[:, f % 2, 0]).then_inc(wd_lo, 1)

            wd_low(0)
            wd_low(1)
            dve.wait_ge(act_lo, 2 * FT)
            dve.wait_ge(dma_ffn_w, 16)
            for p in range(NPAIR):
                dve.wait_ge(td_ready, p + 1)
                nc.vector.tensor_tensor(td_raw[:, p], ps[:, 4 + p, 0:PAIR], block_mask, ALU.mult).then_inc(td_masked, 1)
                for k in W0_AFTER[p]:
                    dve.wait_ge(w0_ready, k + 1)
                    nc.vector.tensor_tensor(w0_raw[:, k], w0_raw[:, k], ps[:, k % 2], ALU.add).then_inc(w0_sum, 1)
            for p in range(NPAIR):
                dve.wait_ge(td_hi, p + 1)
                low(td_st[32:64, p], td_raw[32:64, p], td_st[32:64, p]).then_inc(td_lo, 1)
            for k in range(KD):
                dve.wait_ge(w0_hi, k + 1)
                low(w0_hl[:, 1, k], w0_raw[:, k], w0_hl[:, 0, k]).then_inc(w0_lo, 1)
            dve.wait_ge(bd_hi, 1)
            low(bd_st[64:96], bd_raw[64:96], bd_st[64:96]).then_inc(bd_lo, 1)

            def x2_add(s):
                dve.wait_ge(dma_x2[s], 16)
                for o in range(KD):
                    half = slice(s * HALF, s * HALF + HALF)
                    dve.wait_ge(x2_ready, KD * s + o + 1)
                    nc.vector.scalar_tensor_tensor(x2[:, o, half], ps[:, 4 * s + o], bias0_sb[:, o:o + 1],
                                                   x2[:, o, half], ALU.add, ALU.add).then_inc(x2_done, 1)

            def wc_low(b):
                dve.wait_ge(wc_hi, b + 1)
                low(wc_hl[b % PREP][:, 1], wc_raw[b % WC_RAW][:], wc_hl[b % PREP][:, 0]).then_inc(wc_lo, 1)

            def xs_low(b):
                dve.wait_ge(xs_hi, b + 1)
                low(xs_hl[:, b % 2, 1], x2[:, :, b * SEQ:b * SEQ + SEQ], xs_hl[:, b % 2, 0]).then_inc(xs_lo, 1)

            def c_bias(b):
                dve.wait_ge(c_ready, b + 1)
                if b >= 2:
                    dve.wait_ge(ct_ready, b - 1)
                nc.vector.tensor_tensor(c_tok[:, b % 2], ps[:, b % 2], bias1_sb[:], ALU.add).then_inc(c_done, 1)

            def ct_low(b):
                dve.wait_ge(ct_hi, b + 1)
                cols = slice(b * SEQ, b * SEQ + SEQ)
                low(c_hl[:, 1, :, cols], ps[:, 2 + b % 2].rearrange("p (o t) -> p o t", t=SEQ),
                    c_hl[:, 0, :, cols]).then_inc(ct_lo, 1)

            steps = [0]

            def step(ins):
                steps[0] += 1
                ins.then_inc(top_step, 1)
                dve.wait_ge(top_step, steps[0])

            def route_first8(s):
                dve.wait_ge(score_ready, s + 1)
                step(nc.vector.tensor_copy(score[:], ps[:, 5, 0:4 * EXPERTS].rearrange("p (t e) -> p t e", t=4)))
                for t in range(4):
                    last = nc.vector.max(top8[:, t, 0], score[:, t])
                step(last)
                nc.vector.tensor_tensor(expo[:], score[:], top8[:, :, 0, 0:1].broadcast_to([P, 4, EXPERTS]),
                                        ALU.subtract).then_inc(shifted, 1)
                for t in range(4):
                    last = nc.vector.match_replace(left1[:, t], top8[:, t, 0], score[:, t], NEG)
                step(last)

            def route_next8():
                for t in range(4):
                    last = nc.vector.max(top8[:, t, 1], left1[:, t])
                step(last)
                for t in range(4):
                    last = nc.vector.match_replace(left2[:, t], top8[:, t, 1], left1[:, t], NEG)
                step(last)
                step(nc.vector.tensor_tensor(left2[:], left2[:], score[:], ALU.not_equal))

            def route_gates(s):
                dve.wait_ge(exp_done, s + 1)
                step(nc.vector.tensor_tensor(left1[:], expo[:], left2[:], ALU.mult))
                step(nc.vector.tensor_reduce(gate_sum[:], left1[:], AX_X, ALU.add))
                step(nc.vector.reciprocal(gate_inv[:], gate_sum[:]))
                if s:
                    dve.wait_ge(gate_tr, s)
                for t in range(4):
                    last = nc.vector.tensor_scalar(
                        gate2[:, t], left1[:, t].unsqueeze(1).broadcast_to([P, 2, EXPERTS]),
                        gate_inv[:, t:t + 1], MOE_SCALE, ALU.mult, ALU.mult)
                last.then_inc(gate_done, 1)

            for f in range(2, FT):
                wd_low(f)
                if f in (4, 6, 8):
                    wc_low((f - 4) // 2)
            for s in range(2):
                for o in range(KD):
                    half = slice(s * HALF, s * HALF + HALF)
                    dve.wait_ge(d_hi, KD * s + o + 1)
                    low(d_hl[:, 1, o, half], ps[:, 4 * s + o], d_hl[:, 0, o, half]).then_inc(d_lo, 1)
            dve.wait_ge(wr_hi, 1)
            low(wr_st[:, :, 1], wr_raw[:], wr_st[:, :, 0]).then_inc(wr_lo, 1)
            wc_low(3)
            x2_add(0)
            xs_low(0)
            xs_low(1)
            x2_add(1)
            dve.wait_ge(dma_l1, 32)
            for b in range(BATCH):
                c_bias(b)
                if b + 2 < BATCH:
                    xs_low(b + 2)
                if b:
                    ct_low(b - 1)
                if b == 6:
                    route_first8(0)
            ct_low(BATCH - 1)
            route_next8()
            route_gates(0)

            def hg_gate(n):
                j, s = H_ORDER[n]
                dve.wait_ge(h_ready, n + 1)
                dve.wait_ge(late_banks_free, 2 * (s + 1))
                if n >= 2:
                    dve.wait_ge(hg_hi, n - 1)
                    dve.wait_ge(hg_lo, n - 1)
                nc.vector.tensor_tensor(hg_raw[:, n % 2], ps[:, n % 4], gate_x[:, s],
                                        ALU.mult).then_inc(hg_mul, 1)

            def hg_low(n):
                j, s = H_ORDER[n]
                half = slice(s * HALF, s * HALF + HALF)
                dve.wait_ge(hg_hi, n + 1)
                low(hg[j // 2][:, j % 2, 1, half], hg_raw[:, n % 2], hg[j // 2][:, j % 2, 0, half]).then_inc(hg_lo, 1)

            route_first8(1)
            hg_gate(0)
            hg_gate(1)
            hg_low(0)
            route_next8()
            hg_low(1)
            hg_gate(2)
            route_gates(1)
            hg_low(2)
            hg_gate(3)
            hg_low(3)
            for n in range(4, 2 * JT):
                hg_gate(n)
                if n >= 5:
                    hg_low(n - 1)
            hg_low(2 * JT - 1)
            for n in range(2 * KD):
                o, s = n // 2, n % 2
                half = slice(s * HALF, s * HALF + HALF)
                dve.wait_ge(o_ready, n + 1)
                nc.vector.tensor_tensor(x2[:, o, half], ps[:, 4 + n % 4], x2[:, o, half], ALU.add)\
                    .then_inc(late_banks_free, 1)

        @block.tensor
        def _(pe):
            def mm3(out, w_high, w_low, m_high, m_low, start, stop):
                nc.tensor.matmul(out, w_high, m_high, start=start, stop=False)
                nc.tensor.matmul(out, w_high, m_low, start=False, stop=False)
                return nc.tensor.matmul(out, w_low, m_high, start=False, stop=stop)

            def halves(s):
                return slice(s * HALF, s * HALF + HALF)

            def project(slot, bank, m, s, first=False, part=range(KD)):
                for k in part:
                    if first:
                        pe.wait_ge(x_hi, KD * s + k + 1)
                        pe.wait_ge(x_lo, KD * s + k + 1)
                    mm3(ps[:, 4 * bank + 2 * s + m], w_hl[slot][:, 0, m, k], w_hl[slot][:, 1, m, k],
                        x_hl[:, 0, k, halves(s)], x_hl[:, 1, k, halves(s)], k == 0, False)

            def adapt(slot, bank, m, s):
                for h in range(2):
                    last = nc.tensor.matmul(ps[:, 4 * bank + 2 * s + m, h * PAIR:h * PAIR + PAIR],
                                            b_st[slot][:, m, 2 * s + h], t_st[:, 2 * s + h, m],
                                            start=False, stop=h == 1)
                last.then_inc(up_ready if m else gate_ready, 1)

            pe.wait_ge(warm_set, 1)
            for _ in range(WARM_UP):
                nc.tensor.matmul(ps[:, 7, 0:P], warm[:, 0:P], warm[:, 0:P], start=True, stop=True)
            for k in range(KD):
                pe.wait_ge(w_hi, k + 1)
                pe.wait_ge(w_lo, k + 1)
                pe.wait_ge(x_hi, k + 1)
                pe.wait_ge(x_lo, k + 1)
                for m in range(2):
                    mm3(ps[:, m], w_hl[0][:, 0, m, k], w_hl[0][:, 1, m, k],
                        x_hl[:, 0, k, halves(0)], x_hl[:, 1, k, halves(0)], k == 0, False)
            project(0, 0, 0, 1, first=True)
            project(0, 0, 1, 1, part=range(1))
            pe.wait_ge(dma_a, 16 * A_BY_POOL)
            pe.wait_ge(dma_a_sp, 16 * (BATCH - A_BY_POOL))
            pe.wait_ge(dma_const, 16)
            for m in range(2):
                for k in range(KD):
                    nc.tensor.transpose(ps[:, 4 + m, k * P:k * P + P], a_nat[:, m, k * P:k * P + P],
                                        ident).then_inc(a_tr, 1)
            project(0, 0, 1, 1, part=range(1, KD))
            pe.wait_ge(a_hi, 2)
            pe.wait_ge(a_lo, 2)
            for p in range(NPAIR):
                cols = slice(p * PAIR, p * PAIR + PAIR)
                for k in range(KD):
                    stack = a_st[:, NPAIR * k + p].rearrange("p m h r -> p (m h r)")
                    for h in range(2):
                        last = nc.tensor.matmul(ps[:, 4 + p, 0:PAIR], stack, x_hl[:, h, k, cols],
                                                start=(k == 0 and h == 0), stop=(k == KD - 1 and h == 1))
                last.then_inc(t_ready, 1)

            def adapt_first(s):
                pe.wait_ge(t_hi, 8 * s + 8)
                pe.wait_ge(t_lo, 4 * s + 4)
                for m in range(2):
                    adapt(0, 0, m, s)

            pe.wait_ge(w_hi, KD + 1)
            pe.wait_ge(w_lo, KD + 1)
            for n in range(3):
                pe.wait_ge(t_masked, n + 1)
                project(1, 1, n % 2, n // 2)
            pe.wait_ge(b_hi, 1)
            pe.wait_ge(b_lo, 2)
            adapt_first(0)
            adapt_first(1)
            pe.wait_ge(b_hi, 2)
            pe.wait_ge(b_lo, 4)
            for m in range(2):
                adapt(1, 1, m, 0)
            adapt(1, 1, 0, 1)
            project(1, 1, 1, 1)
            adapt(1, 1, 1, 1)

            def tile_half(f, u, s):
                pe.wait_ge(silu_done, 2 * f + s - 3)
                project(u, u, 0, s)
                if s == 0:
                    pe.wait_ge(b_hi, f + 1)
                    pe.wait_ge(b_lo, 2 * f + 2)
                adapt(u, u, 0, s)
                pe.wait_ge(glu_done, 2 * f + s - 3)
                project(u, u, 1, s)
                adapt(u, u, 1, s)

            with pe.Fori(0, (FT - 3) // 2) as i:
                for u in range(2):
                    f = 2 * i + 2 + u
                    pe.wait_ge(w_hi, KD + f)
                    pe.wait_ge(w_lo, KD + f)
                    tile_half(f, u, 0)
                    tile_half(f, u, 1)
            pe.wait_ge(w_hi, KD + FT - 1)
            pe.wait_ge(w_lo, KD + FT - 1)
            tile_half(FT - 1, 0, 0)
            pe.wait_ge(dma_ad, 16 * BATCH)
            pe.wait_ge(glu_done, 2 * FT - 2)
            for f in range(FT):
                nc.tensor.transpose(ps[:, 4 + f // 4, (f % 4) * P:(f % 4) * P + P],
                                    ad_nat[:, f * P:f * P + P], ident).then_inc(ad_tr, 1)
            tile_half(FT - 1, 0, 1)

            def act_part(f, h, lo, n):
                at0 = f * 2 * T + h * T + lo
                return act[:, at0:at0 + n]

            pe.wait_ge(ad_hi, 3)
            pe.wait_ge(ad_lo, 3)
            for p in range(NPAIR):
                for f in range(FT):
                    pe.wait_ge(act_hi, 2 * f + p // 2 + 1)
                    pe.wait_ge(act_lo, 2 * f + p // 2 + 1)
                    stack = ad_st[:, NPAIR * f + p].rearrange("p c r -> p (c r)")
                    for h in range(2):
                        last = nc.tensor.matmul(ps[:, 4 + p, 0:PAIR], stack,
                                                act_part(f, h, p * PAIR, PAIR),
                                                start=(f == 0 and h == 0), stop=(f == FT - 1 and h == 1))
                last.then_inc(td_ready, 1)
                if p == 0:
                    pe.wait_ge(lora_hi, 2)
                    pe.wait_ge(lora_lo, 2)
                    pe.wait_ge(glu_done, 2 * FT - 1)
                for k in W0_AFTER[p]:
                    if k >= 2:
                        pe.wait_ge(w0_sum, k - 1)
                    cols = slice(k * P, k * P + P)
                    mm3(ps[:, k % 2], la_hl[:, 0, cols], la_hl[:, 1, cols], lb_hl[:, 0], lb_hl[:, 1], True,
                        True).then_inc(w0_ready, 1)

            pe.wait_ge(glu_done, 2 * FT)
            for f in range(FT):
                pe.wait_ge(wd_hi, f + 1)
                pe.wait_ge(wd_lo, f + 1)
                for s in range(2):
                    if f == 0:
                        if s == 0:
                            pe.wait_ge(w0_sum, KD)
                        else:
                            pe.wait_ge(td_masked, NPAIR)
                    for o in range(KD):
                        cols = slice(o * P, o * P + P)
                        last = mm3(ps[:, 4 * s + o], wd_hl[:, f % 2, 0, cols], wd_hl[:, f % 2, 1, cols],
                                   act_part(f, 0, s * HALF, HALF), act_part(f, 1, s * HALF, HALF), f == 0, False)
                        if f == FT - 1:
                            pe.wait_ge(bd_hi, 1)
                            pe.wait_ge(bd_lo, 1)
                            pe.wait_ge(td_hi, NPAIR)
                            pe.wait_ge(td_lo, NPAIR)
                            for h in range(2):
                                last = nc.tensor.matmul(ps[:, 4 * s + o, h * PAIR:h * PAIR + PAIR],
                                                        bd_st[:, 2 * s + h, cols], td_st[:, 2 * s + h],
                                                        start=False, stop=h == 1)
                            last.then_inc(d_ready, 1)
                if f < FT - 1:
                    last.then_inc(down_tiles, 1)

            pe.wait_ge(w0_hi, KD)
            pe.wait_ge(w0_lo, KD)
            for s in range(2):
                pe.wait_ge(d_lo, KD * s + KD)
                for o in range(KD):
                    cols = slice(o * P, o * P + P)
                    for k in range(KD):
                        last = mm3(ps[:, 4 * s + o], w0_hl[:, 0, k, cols], w0_hl[:, 1, k, cols],
                                   d_hl[:, 0, k, halves(s)], d_hl[:, 1, k, halves(s)], k == 0, k == KD - 1)
                    last.then_inc(x2_ready, 1)

            def cond(b):
                pe.wait_ge(xs_hi, b + 1)
                pe.wait_ge(xs_lo, b + 1)
                pe.wait_ge(wc_hi, b + 1)
                if b < DVE_SPLITS:
                    pe.wait_ge(wc_lo, b + 1)
                else:
                    pe.wait_ge(wc_lo_late, b + 1 - DVE_SPLITS)
                if b < 2:
                    pe.wait_ge(x2_done, KD)
                else:
                    pe.wait_ge(c_done, b - 1)
                for k in range(KD):
                    last = mm3(ps[:, b % 2], xs_hl[:, b % 2, 0, k], xs_hl[:, b % 2, 1, k],
                               wc_hl[b % PREP][:, 0, k], wc_hl[b % PREP][:, 1, k], k == 0, k == KD - 1)
                last.then_inc(c_ready, 1)

            def turn(b):
                pe.wait_ge(c_done, b + 1)
                if b >= 2:
                    pe.wait_ge(ct_lo, b - 1)
                for o in range(KD):
                    last = nc.tensor.transpose(ps[:, 2 + b % 2, o * SEQ:o * SEQ + SEQ],
                                               c_tok[:, b % 2, o * P:o * P + P], ident)
                last.then_inc(ct_ready, 1)

            def scores(s):
                pe.wait_ge(ct_hi, 4 * s + 4)
                pe.wait_ge(ct_lo, 4 * s + 4)
                pe.wait_ge(x2_done, 2 * KD)
                pe.wait_ge(wr_hi, 1)
                pe.wait_ge(wr_lo, 1)
                for k in range(KD):
                    for h in range(2):
                        last = nc.tensor.matmul(ps[:, 4], wr_st[:, k].rearrange("p h e -> p (h e)"),
                                                c_hl[:, h, k, halves(s)], start=(k == 0 and h == 0),
                                                stop=(k == KD - 1 and h == 1))
                last.then_inc(s_ready, 1)

            def turn_scores(s):
                pe.wait_ge(s_copied, s + 1)
                for t in range(4):
                    last = nc.tensor.matmul(ps[:, 5, t * EXPERTS:(t + 1) * EXPERTS], s_sb[:, t * P:t * P + P],
                                            ident2, start=True, stop=True)
                last.then_inc(score_ready, 1)

            def turn_gates(s):
                pe.wait_ge(gate_done, s + 1)
                if s:
                    pe.wait_ge(late_banks_free, 2)
                for t in range(4):
                    last = nc.tensor.transpose(ps[:, 6, t * P:t * P + P],
                                               gate2[:, t].rearrange("p c e -> p (c e)"), ident)
                last.then_inc(gate_tr, 1)

            def experts(n, part=range(KD)):
                j, s = H_ORDER[n]
                pe.wait_ge(am_hi, j + 1)
                pe.wait_ge(am_lo, j + 1)
                if n >= 4:
                    pe.wait_ge(hg_mul, n - 3)
                for k in part:
                    last = mm3(ps[:, n % 4], am_hl[:, j % AM_SLOTS, 0, k], am_hl[:, j % AM_SLOTS, 1, k],
                               c_hl[:, 0, k, halves(s)], c_hl[:, 1, k, halves(s)], k == 0, k == KD - 1)
                    if k == KD - 1:
                        last.then_inc(h_ready, 1)

            cond(0)
            for b in range(1, BATCH):
                cond(b)
                if b == 5:
                    scores(0)
                turn(b - 1)
                if b == 6:
                    turn_scores(0)
            pe.wait_ge(c_done, BATCH - 1)
            experts(0, range(1))
            turn(BATCH - 1)
            experts(0, range(1, KD))
            scores(1)
            experts(1)
            turn_scores(1)
            turn_gates(0)
            pe.wait_ge(ct_lo, BATCH)
            experts(2)
            experts(3)
            experts(4)
            experts(5)
            turn_gates(1)
            for n in range(6, 2 * JT):
                experts(n)

            with pe.Fori(0, KD // 2) as i:
                for u in range(2):
                    o = 2 * i + u
                    pe.wait_ge(bm_hi, o + 1)
                    pe.wait_ge(bm_lo, o + 1)
                    for s in range(2):
                        pe.wait_ge(late_banks_free, 2 * o + s + 1)
                        pe.wait_ge(hg_lo, HALF_TAIL + AM_SLOTS * s)
                        for j in range(JT):
                            last = mm3(ps[:, 4 + 2 * u + s], bm_hl[:, u, 0, j], bm_hl[:, u, 1, j],
                                       hg[j // 2][:, j % 2, 0, halves(s)], hg[j // 2][:, j % 2, 1, halves(s)], j == 0, j == JT - 1)
                        last.then_inc(o_ready, 1)


def constants():
    row, col = np.arange(P)[:, None], np.arange(PAIR)[None, :]
    own = (row % 32) // RANK == col // SEQ
    eye = np.eye(P)
    return np.concatenate([LORA_SCALE * own, eye, eye[:, :EXPERTS] + eye[:, EXPERTS:]], 1).astype(np.float32)


def features_first(w, tiles):
    return w.T.reshape(tiles, P, -1).transpose(1, 0, 2)


def kernel(x, itok_B_2_6, condB_coeff, mask_Bx4096x4096_ik1, L0_cond_W_gate, L0_cond_W_up, L0_cond_W_down,
           L0_cond_A_gate, L0_cond_B_gate, L0_cond_A_up, L0_cond_B_up, L0_cond_A_down, L0_cond_B_down,
           L0_ffn_lora_A, L0_ffn_lora_B, L0_ffn_W, L0_ffn_bias, L0_ffn_lora_weights, L1_cond_W, L1_cond_b,
           L1_ffn_A, L1_ffn_B, L1_ffn_Wr):
    import concourse.bacc as bacc
    from concourse.bass_utils import run_bass_kernel_spmd

    def pad_f(w, axis):
        widths = [(0, 0)] * w.ndim
        widths[axis] = (0, FPAD - F)
        return np.pad(w, widths)

    a = {k: np.asarray(v) for k, v in locals().items() if isinstance(v, np.ndarray) or hasattr(v, "dtype")}
    w_gu = np.stack([pad_f(a["L0_cond_W_gate"], 0), pad_f(a["L0_cond_W_up"], 0)])
    w_gu = w_gu.reshape(2, FT, P, KD, P).transpose(1, 4, 0, 3, 2)
    w_dn = pad_f(a["L0_cond_W_down"], 1).T.reshape(FT, P, D)
    b_t = {m: a[f"L0_cond_B_{m}"][0].transpose(0, 2, 1) for m in ("gate", "up", "down")}
    ins = {
        "x_t": features_first(a["x"].reshape(T, D), KD),
        "itok": a["itok_B_2_6"].reshape(1, BATCH),
        "coeff": a["condB_coeff"].reshape(1, BATCH),
        "mask_w": a["mask_Bx4096x4096_ik1"].reshape(BATCH, KD, P, D).transpose(0, 2, 1, 3),
        "w_gu": w_gu,
        "w_dn": w_dn,
        "a_gu": np.stack([a["L0_cond_A_gate"][0], a["L0_cond_A_up"][0]], 2),
        "a_dn": pad_f(a["L0_cond_A_down"][0], 2),
        "b_gu": np.stack([pad_f(b_t["gate"], 2), pad_f(b_t["up"], 2)], 1),
        "b_dn": b_t["down"],
        "lora_a": a["L0_ffn_lora_A"].reshape(P, D),
        "lora_b": a["L0_ffn_lora_B"].transpose(0, 2, 1).reshape(P, D),
        "lora_w": np.repeat(a["L0_ffn_lora_weights"], RANK).reshape(P, 1),
        "w0_t": features_first(a["L0_ffn_W"], KD),
        "bias0": a["L0_ffn_bias"].reshape(KD, P).T,
        "w1_t": features_first(a["L1_cond_W"], KD),
        "bias1": a["L1_cond_b"].reshape(1, D),
        "wr_t": features_first(a["L1_ffn_Wr"], KD),
        "a_moe": a["L1_ffn_A"].transpose(1, 0, 2).reshape(JT, P, KD, P).transpose(0, 3, 2, 1),
        "b_moe": a["L1_ffn_B"].transpose(2, 0, 1).reshape(JT, P, KD, P).transpose(2, 1, 0, 3),
        "consts": constants(),
    }
    ins = {k: np.ascontiguousarray(v) for k, v in ins.items()}
    nc = bacc.Bacc("TRN2", target_bir_lowering=False, num_devices=1)
    args = [nc.dram_tensor(k, v.shape, mybir.dt.from_np(v.dtype), kind="ExternalInput").ap() for k, v in ins.items()]
    out = nc.dram_tensor("out", (KD, P, T), F32, kind="ExternalOutput").ap()
    build(nc, *args, out)
    r = run_bass_kernel_spmd(nc, [ins], core_ids=[0])
    return r.results[0]["out"].reshape(D, T).T.reshape(BATCH, SEQ, D)
```
